# Optimizing a Trainium2 kernel written in Bass

```python
import numpy as np
import jax
import jax.numpy as jnp

def _softmax(x, axis=-1):
    return jax.nn.softmax(x, axis=axis)
def _gelu(x):
    return jax.nn.gelu(x, approximate=True)
def _silu(x):
    return jax.nn.silu(x)
def _sigmoid(x):
    return jax.nn.sigmoid(x)
def _layernorm(x, axis=-1, eps=1e-5):
    m = jnp.mean(x, axis=axis, keepdims=True)
    v = jnp.var(x, axis=axis, keepdims=True)
    return (x - m) / jnp.sqrt(v + eps)
def _scatter_add(tgt, idx, src, axis=0):
    return tgt.at[idx].add(src)
def _segment_sum(src, seg, n):
    return jax.ops.segment_sum(src, seg, n)

kernel_name = 'mk_adj_ffn_d2_adj_256_ad86f7'

def setup_inputs(seed: int = 0):
    np.random.seed(seed)
    _w = jnp.asarray
    def _rec_inputs():
        import jax
        import jax.numpy as jnp
        _gk = jax.random.key(seed)
        x = -0.000929 + 1 * jax.random.normal(jax.random.fold_in(_gk, 1), (4096, 256), jnp.float32)
        _a = jax.random.bernoulli(jax.random.fold_in(_gk, 2), 0.0078125, (4096, 4096))
        _a = jnp.logical_or(_a, jnp.swapaxes(_a, -1, -2))
        _a = jnp.logical_or(_a, jnp.eye(4096, dtype=bool))
        adj = _a
        return x, adj
    x, adj = _rec_inputs()
    def _L0_gnn_setup():
        import jax, jax.numpy as jnp
        import numpy as np
        B, FIN, H, D = (4096, 256, 4, 64)
        key = jax.random.key(seed)
        k1, k2, k3, k4 = jax.random.split(key, 4)
        x = jax.random.normal(k1, (B, FIN), dtype=jnp.float32)
        W = jax.random.normal(k2, (H * D, FIN), dtype=jnp.float32) * (1.0 / np.sqrt(FIN))
        a_src = jax.random.normal(k3, (H, D), dtype=jnp.float32) * 0.1
        a_dst = jax.random.normal(k4, (H, D), dtype=jnp.float32) * 0.1
        attn_mask = jnp.ones((B, B), dtype=bool)
        return {'x': x, 'attn_mask': attn_mask, 'W': W, 'a_src': a_src, 'a_dst': a_dst}
    _L0_gnn_all = _L0_gnn_setup()
    _L0_gnn_in = {k: v for k, v in _L0_gnn_all.items() if k in ('W', 'a_src', 'a_dst', )}
    del _L0_gnn_all

    def _L0_ffn_setup():
        import jax, jax.numpy as jnp
        import numpy as np
        TOP_K = 2
        key = jax.random.key(seed)
        ks = jax.random.split(key, 4)
        B, L, D, H, E = (8, 4096, 256, 1024, 8)
        s = 0.02
        return {'x': jax.random.normal(ks[0], (B, L, D), jnp.float32), 'Wg': jax.random.normal(ks[1], (D, E), jnp.float32) * s, 'bg': jnp.zeros((E,), jnp.float32), 'W1': jax.random.normal(ks[2], (E, D, H), jnp.float32) * s, 'b1': jnp.zeros((E, H), jnp.float32), 'W2': jax.random.normal(ks[3], (E, H, D), jnp.float32) * s, 'b2': jnp.zeros((E, D), jnp.float32)}
    _L0_ffn_all = _L0_ffn_setup()
    _L0_ffn_in = {k: v for k, v in _L0_ffn_all.items() if k in ('Wg', 'bg', 'W1', 'b1', 'W2', 'b2', )}
    del _L0_ffn_all

    def _L1_gnn_setup():
        import jax, jax.numpy as jnp
        import numpy as np
        N = 4096
        IN_F = 256
        OUT_F = 32
        H = 8
        NEG_SLOPE = 0.2
        EDGE_P = 0.004
        key = jax.random.key(seed)
        k1, k2, k3, k4, k5 = jax.random.split(key, 5)
        x = jax.random.normal(k1, (N, IN_F), dtype=jnp.float32)
        adj = jax.random.bernoulli(k2, EDGE_P, (N, N))
        w_scale = np.sqrt(6.0 / (IN_F + OUT_F))
        a_scale = np.sqrt(6.0 / (OUT_F + 1))
        W = jax.random.uniform(k3, (H, IN_F, OUT_F), jnp.float32, -w_scale, w_scale)
        a_src = jax.random.uniform(k4, (H, OUT_F), jnp.float32, -a_scale, a_scale)
        a_dst = jax.random.uniform(k5, (H, OUT_F), jnp.float32, -a_scale, a_scale)
        bias = jnp.zeros((H * OUT_F,), dtype=jnp.float32)
        return {'x': x, 'adj': adj, 'W': W, 'a_src': a_src, 'a_dst': a_dst, 'bias': bias}
    _L1_gnn_all = _L1_gnn_setup()
    _L1_gnn_in = {k: v for k, v in _L1_gnn_all.items() if k in ('W', 'a_src', 'a_dst', 'bias', )}
    del _L1_gnn_all

    def _L1_ffn_setup():
        import jax, jax.numpy as jnp
        import numpy as np
        E = 8
        K = 2
        D = 256
        H = 512
        DOUT = 256
        EPS = 1e-05
        key = jax.random.key(seed)
        ks = jax.random.split(key, 9)
        s = 0.02
        return {'x': jax.random.normal(ks[0], (4, 8192, D), jnp.float32), 'gamma': 1.0 + 0.05 * jax.random.normal(ks[1], (D,), jnp.float32), 'beta': 0.05 * jax.random.normal(ks[2], (D,), jnp.float32), 'Wr': 0.01 * jax.random.normal(ks[3], (D, E), jnp.float32), 'br': jnp.zeros((E,), jnp.float32), 'W1': s * jax.random.normal(ks[4], (E, D, H), jnp.float32), 'b1': s * jax.random.normal(ks[5], (E, H), jnp.float32), 'W2': s * jax.random.normal(ks[6], (E, H, DOUT), jnp.float32), 'b2': s * jax.random.normal(ks[7], (E, DOUT), jnp.float32)}
    _L1_ffn_all = _L1_ffn_setup()
    _L1_ffn_in = {k: v for k, v in _L1_ffn_all.items() if k in ('gamma', 'beta', 'Wr', 'br', 'W1', 'b1', 'W2', 'b2', )}
    del _L1_ffn_all

    return {
        "x": x,
        "adj": adj,
        "L0_gnn_W": _L0_gnn_in["W"],
        "L0_gnn_a_src": _L0_gnn_in["a_src"],
        "L0_gnn_a_dst": _L0_gnn_in["a_dst"],
        "L0_ffn_Wg": _L0_ffn_in["Wg"],
        "L0_ffn_bg": _L0_ffn_in["bg"],
        "L0_ffn_W1": _L0_ffn_in["W1"],
        "L0_ffn_b1": _L0_ffn_in["b1"],
        "L0_ffn_W2": _L0_ffn_in["W2"],
        "L0_ffn_b2": _L0_ffn_in["b2"],
        "L1_gnn_W": _L1_gnn_in["W"],
        "L1_gnn_a_src": _L1_gnn_in["a_src"],
        "L1_gnn_a_dst": _L1_gnn_in["a_dst"],
        "L1_gnn_bias": _L1_gnn_in["bias"],
        "L1_ffn_gamma": _L1_ffn_in["gamma"],
        "L1_ffn_beta": _L1_ffn_in["beta"],
        "L1_ffn_Wr": _L1_ffn_in["Wr"],
        "L1_ffn_br": _L1_ffn_in["br"],
        "L1_ffn_W1": _L1_ffn_in["W1"],
        "L1_ffn_b1": _L1_ffn_in["b1"],
        "L1_ffn_W2": _L1_ffn_in["W2"],
        "L1_ffn_b2": _L1_ffn_in["b2"],
    }

def reference(x, adj, L0_gnn_W, L0_gnn_a_src, L0_gnn_a_dst, L0_ffn_Wg, L0_ffn_bg, L0_ffn_W1, L0_ffn_b1, L0_ffn_W2, L0_ffn_b2, L1_gnn_W, L1_gnn_a_src, L1_gnn_a_dst, L1_gnn_bias, L1_ffn_gamma, L1_ffn_beta, L1_ffn_Wr, L1_ffn_br, L1_ffn_W1, L1_ffn_b1, L1_ffn_W2, L1_ffn_b2):
    import jax
    import jax.numpy as jnp
    def _L0_gnn_ref(x, attn_mask, W, a_src, a_dst):
        import jax, jax.numpy as jnp
        import numpy as np
        B, FIN, H, D = (4096, 256, 4, 64)
        h = (x @ W.T).reshape(B, H, D)
        e_src = jnp.einsum('bhd,hd->bh', h, a_src)
        e_dst = jnp.einsum('bhd,hd->bh', h, a_dst)
        e = jax.nn.leaky_relu(e_src[:, None, :] + e_dst[None, :, :], negative_slope=0.2)
        e = jnp.where(attn_mask[:, :, None], e, -jnp.inf)
        alpha = jax.nn.softmax(e, axis=1)
        out = jnp.einsum('ijh,jhd->ihd', alpha, h).reshape(B, H * D)
        return jax.nn.elu(out)

    def _L0_ffn_ref(x, Wg, bg, W1, b1, W2, b2):
        import jax, jax.numpy as jnp
        import numpy as np
        TOP_K = 2
        B, L, D = x.shape
        E = W1.shape[0]
        xf = x.reshape(-1, D)
        gate_logits = xf @ Wg + bg
        top_w, top_i = jax.lax.top_k(gate_logits, TOP_K)
        top_w = jax.nn.softmax(top_w, axis=-1)
        w_dense = jnp.sum(jax.nn.one_hot(top_i, E, dtype=xf.dtype) * top_w[..., None], axis=1)
        out = jnp.zeros_like(xf)
        for e in range(E):
            h = jax.nn.gelu(xf @ W1[e] + b1[e], approximate=False)
            out = out + w_dense[:, e:e + 1] * (h @ W2[e] + b2[e])
        return out.reshape(B, L, D)

    def _L1_gnn_ref(x, adj, W, a_src, a_dst, bias):
        import jax, jax.numpy as jnp
        import numpy as np
        N = 4096
        IN_F = 256
        OUT_F = 32
        H = 8
        NEG_SLOPE = 0.2
        EDGE_P = 0.004
        n = x.shape[0]
        mask = adj | jnp.eye(n, dtype=bool)
        Wh = jnp.einsum('hif,ni->hnf', W, x)
        e_src = jnp.einsum('hnf,hf->hn', Wh, a_src)
        e_dst = jnp.einsum('hnf,hf->hn', Wh, a_dst)
        e = e_src[:, :, None] + e_dst[:, None, :]
        e = jnp.where(e >= 0, e, NEG_SLOPE * e)
        e = jnp.where(mask[None], e, -jnp.inf)
        alpha = jax.nn.softmax(e, axis=-1)
        out = jnp.einsum('hnm,hmf->hnf', alpha, Wh)
        out = jnp.transpose(out, (1, 0, 2)).reshape(n, -1)
        return out + bias

    def _L1_ffn_ref(x, gamma, beta, Wr, br, W1, b1, W2, b2):
        import jax, jax.numpy as jnp
        import numpy as np
        E = 8
        K = 2
        D = 256
        H = 512
        DOUT = 256
        EPS = 1e-05
        mu = jnp.mean(x, axis=-1, keepdims=True)
        var = jnp.mean(jnp.square(x - mu), axis=-1, keepdims=True)
        xn = (x - mu) * jax.lax.rsqrt(var + EPS) * gamma + beta
        logits = jnp.einsum('bsd,de->bse', xn, Wr) + br
        top_vals, top_idx = jax.lax.top_k(logits, K)
        w = jax.nn.softmax(top_vals, axis=-1)
        w_full = jnp.einsum('bsk,bske->bse', w, jax.nn.one_hot(top_idx, E, dtype=w.dtype))
        y = jnp.zeros(x.shape[:-1] + (DOUT,), x.dtype)
        for e in range(E):
            h = jax.nn.gelu(jnp.einsum('bsd,dh->bsh', xn, W1[e]) + b1[e], approximate=False)
            y_e = jnp.einsum('bsh,hd->bsd', h, W2[e]) + b2[e]
            y = y + y_e * w_full[..., e, None]
        return y

    x = x + _L0_gnn_ref(_layernorm(x, axis=-1), adj, L0_gnn_W, L0_gnn_a_src, L0_gnn_a_dst)
    x = x + _L0_ffn_ref((_layernorm(x, axis=-1))[None], L0_ffn_Wg, L0_ffn_bg, L0_ffn_W1, L0_ffn_b1, L0_ffn_W2, L0_ffn_b2)[0]
    x = x + _L1_gnn_ref(_layernorm(x, axis=-1), adj, L1_gnn_W, L1_gnn_a_src, L1_gnn_a_dst, L1_gnn_bias)
    x = x + _L1_ffn_ref((_layernorm(x, axis=-1))[None], L1_ffn_gamma, L1_ffn_beta, L1_ffn_Wr, L1_ffn_br, L1_ffn_W1, L1_ffn_b1, L1_ffn_W2, L1_ffn_b2)[0]
    return x


_drawn_inputs = setup_inputs


def setup_inputs(seed=0):
    import zlib

    import numpy as np

    out = dict(_drawn_inputs(seed))
    spreads = {'L0_ffn_bg': (0.0, 0.1),
     'L0_ffn_b1': (0.0, 0.1),
     'L0_ffn_b2': (0.0, 0.1),
     'L1_gnn_bias': (0.0, 0.1),
     'L1_ffn_br': (0.0, 0.1)}
    factors = {'L1_ffn_gamma': 6.094, 'L1_ffn_beta': 6.003, 'L1_ffn_b1': 8.0, 'L1_ffn_b2': 4.832}
    for name, (base, spread) in spreads.items():
        noise = np.random.default_rng([zlib.crc32(name.encode()), seed]).standard_normal(out[name].shape)
        drawn = base * np.exp(spread * noise) if base else spread * noise
        out[name] = jnp.asarray(drawn.astype(out[name].dtype))
    for name, factor in factors.items():
        out[name] = (out[name] * factor).astype(out[name].dtype)
    return out
```

```python
from contextlib import ExitStack

import concourse.bass as bass
import numpy as np
from concourse import mybir

F32, F16, F8 = mybir.dt.float32, mybir.dt.float16, mybir.dt.float8e4
U8, U32 = mybir.dt.uint8, mybir.dt.uint32
ALU = mybir.AluOpType
ACT = mybir.ActivationFunctionType
X = mybir.AxisListType.X

P = 128
N = 4096
DM = 256
T = N // (2 * P)
NT = 2 * T
KC = DM // P
E = 8
EPS = 1e-5
MASK_SHIFT = 5
STEEP = 2.0 ** 60
TOP = 2.0 ** 14


class Chain:

    def __init__(self, eng, sem, base=0):
        self.eng, self.sem, self.base, self.n = eng, sem, base, 0

    def link(self, ins, tally=None):
        self.n += 1
        ins.then_inc(self.sem, 1)
        if tally is not None:
            wait_apart(self.eng, tally, self.sem, self.base + self.n)
        else:
            self.eng.wait_ge(self.sem, self.base + self.n)


def wait_apart(eng, tally, sem, value):
    eng.wait_ge(sem, value)
    eng.sem_inc(tally, 1)


def spaces(nc, ctx, tag):
    def sb(name, shape, dt):
        return ctx.enter_context(nc.sbuf_tensor(f"{tag}_{name}", shape, dt))

    def ps(name, shape, dt):
        return ctx.enter_context(nc.psum_tensor(f"{tag}_{name}", shape, dt))

    def sem(name):
        return ctx.enter_context(nc.semaphore(f"{tag}_{name}"))

    return sb, ps, sem


def tokens(x):
    return x.rearrange("(t p b) d -> p t b d", p=P, b=2)


def constants(nc, ident, ident16, eye, iota8):
    with ExitStack() as ctx:
        sb, _, sem = spaces(nc, ctx, "const")
        eye32 = sb("eye32", [P, 4 * P], F32)
        made = sem("made")
        block = ctx.enter_context(nc.Block())

        @block.gpsimd
        def _(pool):
            nc.gpsimd.memset(ident[:], 0.0).then_inc(made, 1)
            nc.gpsimd.memset(ident16[:], 0.0).then_inc(made, 1)
            nc.gpsimd.memset(eye32[:], 0.0).then_inc(made, 1)
            nc.gpsimd.iota(iota8[:], pattern=[[1, E]], base=0, channel_multiplier=0,
                           allow_small_or_imprecise_dtypes=True).then_inc(made, 1)
            pool.wait_ge(made, 4)
            for m in (ident, ident16):
                nc.gpsimd.affine_select(out=m[:], in_=m[:], compare_op=ALU.not_equal, fill=1.0, base=0,
                                        pattern=[[-1, P]], channel_multiplier=1).then_inc(made, 1)
            ev = eye32[:].rearrange("p (i b) -> p i b", b=2)
            nc.gpsimd.affine_select(out=ev, in_=ev, compare_op=ALU.not_equal, fill=0.125, base=0,
                                    pattern=[[-1, 2 * P], [1, 2]], channel_multiplier=2).then_inc(made, 1)
            pool.wait_ge(made, 7)
            nc.gpsimd.tensor_copy(eye[:], eye32[:], saturate=False).then_inc(made, 1)
            pool.wait_ge(made, 8)


def transpose_mask(nc, tally, adj, mask_t, ident16):
    G, A = 8, 4
    adj_v = adj.rearrange("(g a q) j -> g a q j", a=A, q=P)
    with ExitStack() as ctx:
        sb, ps, sem = spaces(nc, ctx, "mask")
        rows = sb("rows", [P, A, N], U8)
        blk = sb("blk", [P, 2, T, 2 * A * P], U8)
        pt = ps("pt", [P, 2, T, P], F16)
        rows_loaded = [sem(f"rows_loaded{a}") for a in range(A)]
        transposed = sem("transposed")
        shifted = sem("shifted")
        stored = [sem(f"stored{k}") for k in range(2)]
        block = ctx.enter_context(nc.Block())

        @block.sync
        def _(sp):
            with sp.Fori(0, G) as g:
                for a in range(A):
                    wait_apart(sp, tally, transposed, g * A + (a + 1))
                    sp.dma_start(rows[:, a, :], adj_v[bass.ds(g, 1), a]).then_inc(rows_loaded[a], 16)

        @block.tensor
        def _(pe):
            pe.sem_inc(transposed, A)
            with pe.Fori(0, G) as g:
                for a in range(A):
                    pe.wait_ge(rows_loaded[a], g * 16 + 16)
                    pe.wait_ge(shifted, g * A + (a + 1))
                    pairs = rows[:, a, :].bitcast(F16)
                    for t in range(T):
                        last = nc.tensor.transpose(pt[:, a % 2, t, :], pairs[:, t * P:(t + 1) * P], ident16[:])
                    last.then_inc(transposed, 1)

        @block.vector
        def _(dve):
            dve.sem_inc(shifted, 2)
            with dve.Fori(0, G // 2) as g2:
                for k in range(2):
                    for a in range(A):
                        dve.wait_ge(transposed, g2 * 2 * A + (A + k * A + a + 1))
                        if a == 0:
                            dve.wait_ge(stored[k], g2 * 16 + 16)
                        nc.vector.tensor_scalar(
                            blk[:, k, :, 2 * P * a:2 * P * (a + 1)].bitcast(U32), pt[:, a % 2].bitcast(U32),
                            MASK_SHIFT, None, ALU.logical_shift_left).then_inc(shifted, 1)

        @block.scalar
        def _(act):
            act.sem_inc(stored[0], 16)
            act.sem_inc(stored[1], 16)
            with act.Fori(0, G // 2) as g2:
                for k in range(2):
                    act.wait_ge(shifted, g2 * 2 * A + (2 + (k + 1) * A))
                    width = 2 * A * P
                    act.dma_start(mask_t[:, :, bass.ds(g2 * 2 * width + k * width, width)], blk[:, k]).then_inc(stored[k], 16)
            for k in range(2):
                act.wait_ge(stored[k], 16 + 16 * (G // 2))


def add_diagonal(nc, tally, mask_t, eye):
    with ExitStack() as ctx:
        sb, _, sem = spaces(nc, ctx, "diag")
        W = 4 * P
        d = sb("d", [P, T, W], U8)
        loaded, ored, stored = sem("loaded"), sem("ored"), sem("stored")
        block = ctx.enter_context(nc.Block())

        @block.sync
        def _(sp):
            for t in range(T):
                sp.dma_start(d[:, t, :], mask_t[:, t, t * W:(t + 1) * W]).then_inc(loaded, 16)
            sp.wait_ge(ored, 1)
            for t in range(T):
                sp.dma_start(mask_t[:, t, t * W:(t + 1) * W], d[:, t, :]).then_inc(stored, 16)
            sp.wait_ge(stored, 16 * T)

        @block.vector
        def _(dve):
            dve.wait_ge(loaded, 16 * T)
            e = eye[:].bitcast(U32)
            nc.vector.tensor_tensor(d[:].bitcast(U32), d[:].bitcast(U32),
                                    e.rearrange("p (a w) -> p a w", a=1).broadcast_to([P, T, W // 4]),
                                    ALU.bitwise_or).then_inc(ored, 1)


def project(nc, tally, tag, H, D, x, w_rows, w_cols, a_src, a_dst, ident, s_rows, UV, NEGD, BIGD, AL, BE):
    D1 = D + 1
    C = DM + 2 * H
    xv = tokens(x)
    with ExitStack() as ctx:
        sb, ps, sem = spaces(nc, ctx, tag)
        WR = sb("WR", [P, KC, DM], F32)
        WC = sb("WC", [P, KC, C], F32)
        AB = sb("AB", [P, KC, 2 * H], F32)
        XS = sb("XS", [P, 2, 2, DM], F32)
        XN = sb("XN", [P, 2, 2, DM], F32)
        XT = sb("XT", [P, 2, KC, 2, P], F32)
        ST = sb("ST", [P, 2, 2, 6], F32)
        MV = sb("MV", [P, 2, 2, 2], F32)
        SD = sb("SDEV", [P, 2, 2], F32)
        RS = sb("RS", [P, 2, 2], F32)
        HB = sb("HB", [P, NT, DM], F32)
        SC = sb("SC", [P, NT, 2 * H], F32)
        SR = sb("SR", [H, N], F32)
        MX = sb("MX", [P, H + 1], F32)
        MA = sb("MA", [P, H + 1], F32)
        KA = sb("KA", [P, 3], F32)
        EPT = sb("EPT", [P, 1], F32)
        Z = sb("Z", [P, 4, NT, H], F32)
        EX = sb("EX", [P, 2, NT, H], F32)
        TM = sb("TM", [P, 2, NT, D1], F32)
        pt = ps("pt", [P, 2, 4, P], F32)
        ph = ps("ph", [P, 2, 2, 512], F32)
        pr = ps("pr", [P, 2, 512], F32)
        w_loaded, zeroed, w_turned, w_copied, folded, w_ready = (sem(n) for n in
            ("w_loaded", "zeroed", "w_turned", "w_copied", "folded", "w_ready"))
        x_loaded = [sem(f"x_loaded{k}") for k in range(2)]
        stats, std, normed, turned, xt_ready, projected, h_out, row_out, dve_chain = (sem(n) for n in
            ("stats", "std", "normed", "turned", "xt_ready", "projected", "h_out", "row_out", "dve_chain"))
        maxes, all_max, args, exps, scaled, hi_done, rows_stored = (sem(n) for n in
            ("maxes", "all_max", "args", "exps", "scaled", "hi_done", "rows_stored"))
        block = ctx.enter_context(nc.Block())
        by_rows = w_rows is not None
        n_w = KC + 2 * H

        @block.sync
        def _(sp):
            for c in range(KC):
                if by_rows:
                    sp.dma_start(WR[:, c, :], w_rows[c * P:(c + 1) * P, :]).then_inc(w_loaded, 16)
                else:
                    sp.dma_start(WC[:, c, 0:DM].rearrange("p (h f) -> p h f", h=H),
                                 w_cols[:, c * P:(c + 1) * P, :].rearrange("h p f -> p h f")).then_inc(w_loaded, 16)
            sp.wait_ge(zeroed, 1)
            for k, a in enumerate((a_src, a_dst)):
                for h in range(H):
                    c, r = divmod(h * D, P)
                    sp.dma_start(AB[r:r + D, c, k * H + h:k * H + h + 1], a[h:h + 1, :].rearrange("a d -> d a")).then_inc(w_loaded, 16)
            with sp.Fori(0, T // 2) as i:
                for k in range(2):
                    wait_apart(sp, tally, normed, i * 2 + (k + 1))
                    sp.dma_start(XS[:, k], xv[:, bass.ds(i * 2 + k, 1)]).then_inc(x_loaded[k], 16)
            sp.wait_ge(row_out, 2 + T)
            sp.dma_start(s_rows, SR[:]).then_inc(rows_stored, 16)
            sp.wait_ge(rows_stored, 16)

        @block.gpsimd
        def _(pool):
            nc.gpsimd.memset(AB[:], 0.0).then_inc(zeroed, 1)
            pool.wait_ge(maxes, 1)
            nc.gpsimd.partition_all_reduce(MA[:], MX[:], P, bass.bass_isa.ReduceOp.max).then_inc(all_max, 1)

        @block.tensor
        def _(pe):
            pe.sem_inc(turned, 2)
            pe.sem_inc(projected, 2)
            pe.wait_ge(w_loaded, 16 * n_w)
            for c in range(KC):
                for c2 in range(KC):
                    src = WR[:, c, c2 * P:(c2 + 1) * P] if by_rows else WC[:, c, c2 * P:(c2 + 1) * P]
                    last = nc.tensor.transpose(pt[:, c, c2, :], src, ident[:])
            last.then_inc(w_turned, 1)
            pe.wait_ge(w_copied, 1)
            for c in range(KC):
                for c2 in range(KC):
                    last = nc.tensor.matmul(pr[:, c, 0:2 * H], WR[:, c2, c * P:(c + 1) * P], AB[:, c2, :],
                                            start=c2 == 0, stop=c2 == KC - 1)
            last.then_inc(folded, 1)
            pe.wait_ge(w_ready, 1)
            with pe.Fori(0, T // 2) as i:
                for k in range(2):
                    pe.wait_ge(normed, i * 2 + (2 + k + 1))
                    pe.wait_ge(xt_ready, i * 2 + (k + 1))
                    for c in range(KC):
                        for b in range(2):
                            last = nc.tensor.transpose(pt[:, k, 2 * c + b, :], XN[:, k, b, c * P:(c + 1) * P], ident[:])
                    last.then_inc(turned, 1)
                for k in range(2):
                    pe.wait_ge(xt_ready, i * 2 + (2 + k + 1))
                    pe.wait_ge(h_out, i * 2 + (k + 1))
                    pe.wait_ge(row_out, i * 2 + (k + 1))
                    for b in range(2):
                        for c in range(KC):
                            nc.tensor.matmul(ph[:, k, b, 0:C], XT[:, k, c, b, :], WC[:, c, :], start=c == 0, stop=c == KC - 1)
                    for c in range(KC):
                        last = nc.tensor.matmul(pr[0:H, k, 0:2 * P], WC[:, c, DM:DM + H],
                                                XT[:, k, c].rearrange("p b m -> p (b m)"), start=c == 0, stop=c == KC - 1)
                    last.then_inc(projected, 1)

        @block.scalar
        def _(act):
            act.sem_inc(xt_ready, 2)
            act.sem_inc(row_out, 2)
            act.wait_ge(w_turned, 1)
            for c in range(KC):
                for c2 in range(KC):
                    dst = WC[:, c2, c * P:(c + 1) * P] if by_rows else WR[:, c2, c * P:(c + 1) * P]
                    last = nc.scalar.copy(dst, pt[:, c, c2, :])
            last.then_inc(w_copied, 1)
            act.wait_ge(folded, 1)
            nc.scalar.copy(WC[:, :, DM:C], pr[:, :, 0:2 * H]).then_inc(w_ready, 1)
            with act.Fori(0, T // 2) as i:
                for k in range(2):
                    act.wait_ge(stats, i * 2 + (k + 1))
                    nc.scalar.activation(SD[:, k, :], MV[:, k, :, 1], ACT.Sqrt, bias=EPT[:, 0:1]).then_inc(std, 1)
                for k in range(2):
                    act.wait_ge(turned, i * 2 + (2 + k + 1))
                    act.wait_ge(projected, i * 2 + (k + 1))
                    nc.scalar.copy(XT[:, k].rearrange("p c b m -> p (c b) m"), pt[:, k]).then_inc(xt_ready, 1)
                for k in range(2):
                    act.wait_ge(projected, i * 2 + (2 + k + 1))
                    nc.scalar.copy(SR[:, bass.ds(i * 4 * P + k * 2 * P, 2 * P)].rearrange("h (m b) -> h b m", b=2),
                                   pr[0:H, k, 0:2 * P].rearrange("h (b m) -> h b m", b=2)).then_inc(row_out, 1)
            act.wait_ge(args, 1)
            nc.scalar.activation(EX[:, 0], Z[:, 1], ACT.Exp)
            nc.scalar.activation(EX[:, 1], Z[:, 1], ACT.Exp, scale=0.2)
            nc.scalar.activation(AL[:], Z[:, 2], ACT.Exp)
            nc.scalar.activation(BE[:], Z[:, 3], ACT.Exp).then_inc(exps, 1)
            for n in range(2 * H):
                h, g = divmod(n, 2)
                act.wait_ge(scaled, n + 1)
                nc.scalar.copy(UV[:, h, :, 2 * g, :], TM[:, n % 2]).then_inc(hi_done, 1)

        @block.vector
        def _(dve):
            dve.sem_inc(normed, 2)
            dve.sem_inc(h_out, 2)
            nc.vector.memset(EPT[:], EPS).then_inc(dve_chain, 1)
            dve.wait_ge(dve_chain, 1)
            links = 6
            with dve.Fori(0, T // 2) as i:
                ch = Chain(dve, dve_chain, dve.snap(i * links + 1))
                for k in range(2):
                    dve.wait_ge(x_loaded[k], i * 16 + 16)
                    nc.vector.bn_stats(ST[:, k, 0, :], XS[:, k, 0, :])
                    ch.link(nc.vector.bn_stats(ST[:, k, 1, :], XS[:, k, 1, :]), tally=tally)
                    nc.vector.bn_aggr(MV[:, k, 0, :], ST[:, k, 0, :])
                    nc.vector.bn_aggr(MV[:, k, 1, :], ST[:, k, 1, :]).then_inc(stats, 1)
                for k in range(2):
                    dve.wait_ge(std, i * 2 + (k + 1))
                    ch.link(nc.vector.reciprocal(RS[:, k, :], SD[:, k, :]))
                    dve.wait_ge(turned, i * 2 + (k + 1))
                    ch.link(nc.vector.tensor_scalar(XN[:, k, 0, :], XS[:, k, 0, :], MV[:, k, 0, 0:1], RS[:, k, 0:1], ALU.subtract, ALU.mult))
                    nc.vector.tensor_scalar(XN[:, k, 1, :], XS[:, k, 1, :], MV[:, k, 1, 0:1], RS[:, k, 1:2],
                                            ALU.subtract, ALU.mult).then_inc(normed, 1)
                for k in range(2):
                    dve.wait_ge(projected, i * 2 + (2 + k + 1))
                    nc.vector.tensor_copy(HB[:, bass.ds(i * 4 + 2 * k, 2), :], ph[:, k, :, 0:DM])
                    nc.vector.tensor_copy(SC[:, bass.ds(i * 4 + 2 * k, 2), :], ph[:, k, :, DM:C]).then_inc(h_out, 1)
                assert ch.n == links
            ch = Chain(dve, dve_chain, 1 + links * (T // 2))
            dve.wait_ge(h_out, 2 + T)
            nc.vector.tensor_reduce(MX[:, 0:H], SC[:, :, H:2 * H].rearrange("p n h -> p h n"), X, ALU.max)
            nc.vector.tensor_reduce(MX[:, H:H + 1], HB[:].rearrange("p n d -> p (n d)"), X, ALU.max,
                                    apply_absolute_value=True).then_inc(maxes, 1)
            nc.vector.tensor_scalar(NEGD[:], SC[:, :, H:2 * H], -1.0, None, ALU.mult)
            nc.vector.tensor_scalar(BIGD[:], SC[:, :, H:2 * H], STEEP, None, ALU.mult)
            dve.wait_ge(all_max, 1)
            dmax = MA[:, 0:H].rearrange("p (a h) -> p a h", a=1).broadcast_to([P, NT, H])
            nc.vector.tensor_tensor(Z[:, 1], SC[:, :, H:2 * H], dmax, ALU.subtract)
            ch.link(nc.vector.tensor_tensor(Z[:, 0], SC[:, :, 0:H], dmax, ALU.add))
            nc.vector.tensor_scalar(Z[:, 2], Z[:, 0], 0.8, 0.0, ALU.mult, ALU.min)
            ch.link(nc.vector.tensor_scalar(Z[:, 3], Z[:, 0], -0.8, 0.0, ALU.mult, ALU.min))
            dve.sem_inc(args, 1)
            ch.link(nc.vector.tensor_scalar(KA[:, 0:1], MA[:, H:H + 1], 1.0, None, ALU.max))
            ch.link(nc.vector.reciprocal(KA[:, 1:2], KA[:, 0:1]))
            ch.link(nc.vector.tensor_scalar(KA[:, 2:3], KA[:, 1:2], TOP, None, ALU.mult))
            dve.wait_ge(exps, 1)
            ch.link(nc.vector.tensor_scalar(EX[:], EX[:], KA[:, 2:3], None, ALU.mult))

            def scale(n):
                h, g = divmod(n, 2)
                if n >= 2:
                    dve.wait_ge(hi_done, n - 1)
                e = EX[:, g, :, h:h + 1]
                nc.vector.tensor_copy(TM[:, n % 2, :, D:D1], e)
                nc.vector.tensor_tensor(TM[:, n % 2, :, 0:D], HB[:, :, h * D:(h + 1) * D], e.broadcast_to([P, NT, D]),
                                        ALU.mult).then_inc(scaled, 1)

            def low(n):
                h, g = divmod(n, 2)
                dve.wait_ge(hi_done, n + 1)
                dve.wait_ge(scaled, n + 1)
                ch.link(nc.vector.tensor_tensor(UV[:, h, :, 2 * g + 1, :], TM[:, n % 2], UV[:, h, :, 2 * g, :], ALU.subtract))

            scale(0)
            for n in range(1, 2 * H):
                scale(n)
                low(n - 1)
            low(2 * H - 1)


def attention(nc, tally, tag, H, D, IB, s_rows, mask_t, UV, NEGD, BIGD, AL, BE, OUT):
    D1 = D + 1
    W = 2 * D1
    NI = IB // P
    NB = N // IB
    PER = NI // 4
    U = 16
    NS, NM, NSB = 4, 4, 4
    with ExitStack() as ctx:
        sb, ps, sem = spaces(nc, ctx, tag)
        MB = sb("MB", [P, T, 2 * IB], U8)
        SB = sb("SB", [P, NSB, IB], F32)
        SS = sb("SS", [P, NS, 2 * IB], U8)
        M1 = sb("M1", [P, NM, 2 * IB], U8)
        OE = sb("OE", [P, 2, NI, 3, 2, D1], F32)
        R = sb("R", [P, NI, 3, D1], F32)
        TA = sb("TA", [P, NI, D1], F32)
        TB = sb("TB", [P, NI, D1], F32)
        TC = sb("TC", [P, NI, D1], F32)
        po = ps("po", [P, 2, 4, 512], F32)
        mask_loaded = [sem(f"mask_loaded{g}") for g in range(4)]
        s_loaded = [sem(f"s_loaded{k}") for k in range(NSB)]
        stepped_act, stepped_dve, summed, masked, evacuated, combined, chain = (sem(n) for n in
            ("stepped_act", "stepped_dve", "summed", "masked", "evacuated", "combined", "chain"))
        C_SUM, C_MASKED, C_EV, C_COMB = U * H, U * NSB, 2, 2
        block = ctx.enter_context(nc.Block())

        @block.sync
        def _(sp):
            with sp.Fori(0, NB) as ib:
                iu = sp.snap(ib * (U * H))
                def rows(h):
                    wait_apart(sp, tally, masked, iu + U * (h + 1))
                    sp.dma_start(SB[:, h % NSB, :], s_rows[h:h + 1, bass.ds(ib * IB, IB)].broadcast_to([P, IB])).then_inc(s_loaded[h % NSB], 16)

                for h in range(NSB - 1):
                    rows(h)
                for g in range(4):
                    wait_apart(sp, tally, summed, iu + (U * (H - 1) + 4 * (g + 1)))
                    sp.dma_start(MB[:, 4 * g:4 * g + 4, :], mask_t[:, 4 * g:4 * g + 4, bass.ds(ib * 2 * IB, 2 * IB)]).then_inc(mask_loaded[g], 16)
                for h in range(NSB - 1, H):
                    rows(h)

        @block.scalar
        def _(act):
            act.sem_inc(evacuated, C_EV)
            with act.Fori(0, NB) as ib:
                iu, ih, isl = act.snap(ib * (U * H)), act.snap(ib * H), act.snap(ib * (16 * H // NSB))
                def evacuate(h):
                    act.wait_ge(summed, iu + (C_SUM + U * (h + 1)))
                    act.wait_ge(combined, ih + (h + 1))
                    nc.scalar.copy(OE[:, h % 2].rearrange("p (a n) g l d -> p a (n g l d)", n=PER),
                                   po[:, h % 2, :, 0:PER * 3 * W]).then_inc(evacuated, 1)

                for h in range(H):
                    act.wait_ge(s_loaded[h % NSB], isl + 16 * (h // NSB + 1))
                    for t in range(T):
                        u = U * h + t
                        wait_apart(act, tally, masked, iu + (C_MASKED + u - NS + 1))
                        nc.scalar.activation(SS[:, u % NS, :].bitcast(F8).rearrange("p (i b) -> p b i", b=2)[:, 0, :], SB[:, h % NSB, :],
                                             ACT.Sigmoid, bias=BIGD[:, 2 * t, h:h + 1], scale=STEEP, saturate=False).then_inc(stepped_act, 1)
                        if t == 4 and h > 0:
                            evacuate(h - 1)
                evacuate(H - 1)

        @block.vector
        def _(dve):
            dve.sem_inc(masked, C_MASKED)
            dve.sem_inc(combined, C_COMB)
            links = 6 * H
            with dve.Fori(0, NB) as ib:
                iu, ih, isl, it = dve.snap(ib * (U * H)), dve.snap(ib * H), dve.snap(ib * (16 * H // NSB)), dve.snap(ib * NI)
                ch = Chain(dve, chain, dve.snap(ib * links))

                def step(u):
                    h, t = divmod(u, U)
                    if t == 0:
                        dve.wait_ge(s_loaded[h % NSB], isl + 16 * (h // NSB + 1))
                    dve.wait_ge(masked, iu + (C_MASKED + u - NS + 1))
                    nc.vector.tensor_scalar(SS[:, u % NS, :].rearrange("p (i b) -> p b i", b=2)[:, 1, :], SB[:, h % NSB, :],
                                            NEGD[:, 2 * t + 1, h:h + 1], float(1 << MASK_SHIFT), ALU.is_gt, ALU.mult).then_inc(stepped_dve, 1)

                def mask(u):
                    h, t = divmod(u, U)
                    dve.wait_ge(stepped_dve, iu + (u + 1))
                    dve.wait_ge(stepped_act, iu + (u + 1))
                    dve.wait_ge(summed, iu + (C_SUM + u - NM + 1))
                    if h == 0 and t % 4 == 0:
                        dve.wait_ge(mask_loaded[t // 4], ib * 16 + 16)
                    nc.vector.tensor_tensor(M1[:, u % NM, :].bitcast(U32), SS[:, u % NS, :].bitcast(U32), MB[:, t, :].bitcast(U32),
                                            ALU.bitwise_and).then_inc(masked, 1)

                def combine(h):
                    dve.wait_ge(evacuated, ih + (C_EV + h + 1))
                    al = AL[:, bass.ds(it, NI), h:h + 1].broadcast_to([P, NI, D1])
                    be = BE[:, bass.ds(it, NI), h:h + 1].broadcast_to([P, NI, D1])
                    ch.link(nc.vector.tensor_tensor(R[:], OE[:, h % 2, :, :, 0, :], OE[:, h % 2, :, :, 1, :], ALU.add))
                    dve.sem_inc(combined, 1)
                    ch.link(nc.vector.tensor_tensor(TB[:], R[:, :, 2, :], R[:, :, 1, :], ALU.subtract))
                    nc.vector.tensor_tensor(TA[:], R[:, :, 0, :], al, ALU.mult)
                    ch.link(nc.vector.tensor_tensor(TC[:], TB[:], be, ALU.mult))
                    ch.link(nc.vector.tensor_tensor(TB[:], TA[:], TC[:], ALU.add))
                    ch.link(nc.vector.reciprocal(TA[:, :, 0:1], TB[:, :, D:D1]))
                    ch.link(nc.vector.tensor_tensor(OUT[:, bass.ds(it, NI), h * D:(h + 1) * D], TB[:, :, 0:D],
                                                    TA[:, :, 0:1].broadcast_to([P, NI, D]), ALU.mult))

                step(0)
                for u in range(U * H):
                    if u + 1 < U * H:
                        step(u + 1)
                    mask(u)
                    if u % U == 8 and u > U:
                        combine(u // U - 1)
                combine(H - 1)
                assert ch.n == links

        @block.tensor
        def _(pe):
            pe.sem_inc(summed, C_SUM)
            m1 = M1[:].bitcast(F8).rearrange("p s (q m bi bj) -> p s q bi bj m", bi=2, bj=2, m=P)
            mb = MB[:].bitcast(F8).rearrange("p t (q m bi bj) -> p t q bi bj m", bi=2, bj=2, m=P)
            with pe.Fori(0, NB) as ib:
                iu, ih = pe.snap(ib * (U * H)), pe.snap(ib * H)
                for h in range(H):
                    pe.wait_ge(evacuated, ih + (h + 1))
                    for t in range(T):
                        u = U * h + t
                        wait_apart(pe, tally, masked, iu + (C_MASKED + u + 1))
                        for bj in range(2):
                            j = 2 * t + bj
                            uv = UV[:, h, j].rearrange("p g d -> p (g d)")
                            for k in range(NI):
                                q, bi = divmod(k, 2)
                                bank, at = divmod(k, PER)
                                o = po[:, h % 2, bank, at * 3 * W:(at + 1) * 3 * W]
                                nc.tensor.matmul(o[:, 0:2 * W], m1[:, u % NM, q, bi, bj], uv, start=j == 0 and at == 0,
                                                 stop=j == NT - 1, skip_group_check=True)
                                last = nc.tensor.matmul(o[:, 2 * W:3 * W], mb[:, t, q, bi, bj], uv[:, W:2 * W], start=False,
                                                        stop=j == NT - 1, skip_group_check=True)
                        last.then_inc(summed, 1)


def residual_norm(nc, tally, tag, x, OUT, elu, bias, gamma, beta, ident, Y, XT):
    affine = gamma is not None
    norms = 2 if affine else 1
    xv = tokens(x)
    with ExitStack() as ctx:
        sb, ps, sem = spaces(nc, ctx, tag)
        EL = sb("EL", [P, NT, DM], F32) if elu else None
        BI, GA, BT = (sb(n, [P, DM], F32) for n in ("BI", "GA", "BT")) if affine else (None, None, None)
        EPT = sb("EPT", [P, 1], F32)
        XS = sb("XS", [P, 2, 2, DM], F32)
        TT = sb("TT", [P, 2, DM], F32)
        XN = sb("XN", [P, 2, 2, DM], F32)
        ST = sb("ST", [P, 2, 6], F32)
        MV = sb("MV", [P, 2, 2], F32)
        SD = sb("SDEV", [P, 2], F32)
        RS = sb("RS", [P, 2], F32)
        pt = ps("pt", [P, 2, 4, P], F32)
        n_const = 3 if affine else 0
        const_loaded, clipped, elu_done, added, stats, std, normed, turned, xt_ready, chain = (sem(n) for n in
            ("const_loaded", "clipped", "elu_done", "added", "stats", "std", "normed", "turned", "xt_ready", "chain"))
        x_loaded = [sem(f"x_loaded{k}") for k in range(2)]
        block = ctx.enter_context(nc.Block())

        @block.sync
        def _(sp):
            if affine:
                for dst, src in ((BI, bias), (GA, gamma), (BT, beta)):
                    sp.dma_start(dst[:], src.rearrange("(a e) -> a e", a=1).broadcast_to([P, DM])).then_inc(const_loaded, 16)
            with sp.Fori(0, T // 2) as i:
                for k in range(2):
                    wait_apart(sp, tally, added, i * 2 + (k + 1))
                    sp.dma_start(XS[:, k], xv[:, bass.ds(i * 2 + k, 1)]).then_inc(x_loaded[k], 16)

        @block.scalar
        def _(act):
            act.sem_inc(xt_ready, 2)
            if elu:
                act.wait_ge(clipped, 1)
                nc.scalar.activation(EL[:], EL[:], ACT.Exp).then_inc(elu_done, 1)
            with act.Fori(0, T // 2) as i:
                for k in range(2):
                    for m in range(norms):
                        act.wait_ge(stats, i * (2 * norms) + (k * norms + m + 1))
                        nc.scalar.activation(SD[:], MV[:, :, 1], ACT.Sqrt, bias=EPT[:, 0:1]).then_inc(std, 1)
                    act.wait_ge(turned, i * 2 + (2 + k + 1))
                    nc.scalar.copy(XT[:, :, bass.ds(i * 4 + 2 * k, 2), :],
                                   pt[:, k].rearrange("p (c b) m -> p c b m", c=KC)).then_inc(xt_ready, 1)

        @block.tensor
        def _(pe):
            pe.sem_inc(turned, 2)
            with pe.Fori(0, T // 2) as i:
                for k in range(2):
                    pe.wait_ge(normed, i * 2 + (k + 1))
                    pe.wait_ge(xt_ready, i * 2 + (k + 1))
                    for c in range(KC):
                        for b in range(2):
                            last = nc.tensor.transpose(pt[:, k, 2 * c + b, :], XN[:, k, b, c * P:(c + 1) * P], ident[:])
                    last.then_inc(turned, 1)

        @block.vector
        def _(dve):
            dve.sem_inc(added, 2)
            ch = Chain(dve, chain)
            ch.link(nc.vector.memset(EPT[:], EPS))
            if elu:
                nc.vector.tensor_scalar(EL[:], OUT[:], 0.0, None, ALU.min).then_inc(clipped, 1)
                dve.wait_ge(elu_done, 1)
            else:
                dve.wait_ge(const_loaded, 16 * n_const)
            base = ch.n
            links = 2 * (10 if affine else 4)
            with dve.Fori(0, T // 2) as i:
                ch = Chain(dve, chain, dve.snap(i * links + base))
                for k in range(2):
                    pair = bass.ds(i * 4 + 2 * k, 2)
                    dve.wait_ge(x_loaded[k], i * 16 + 16)
                    if elu:
                        ch.link(nc.vector.scalar_tensor_tensor(TT[:], EL[:, pair, :], -1.0, XS[:, k], ALU.add, ALU.add))
                        ch.link(nc.vector.scalar_tensor_tensor(Y[:, pair, :], OUT[:, pair, :], 0.0, TT[:], ALU.max, ALU.add))
                    else:
                        ch.link(nc.vector.tensor_tensor(TT[:], OUT[:, pair, :], BI[:].rearrange("p (a d) -> p a d", a=1).broadcast_to([P, 2, DM]), ALU.add))
                        ch.link(nc.vector.tensor_tensor(Y[:, pair, :], TT[:], XS[:, k], ALU.add))
                    dve.sem_inc(added, 1)
                    for m in range(norms):
                        last_norm = m == norms - 1
                        src = [Y[:, bass.ds(i * 4 + 2 * k + b, 1), :].rearrange("p a d -> p (a d)") if m == 0 else TT[:, b, :] for b in range(2)]
                        nc.vector.bn_stats(ST[:, 0, :], src[0])
                        ch.link(nc.vector.bn_stats(ST[:, 1, :], src[1]), tally=tally)
                        nc.vector.bn_aggr(MV[:, 0, :], ST[:, 0, :])
                        nc.vector.bn_aggr(MV[:, 1, :], ST[:, 1, :]).then_inc(stats, 1)
                        dve.wait_ge(std, i * (2 * norms) + (k * norms + m + 1))
                        ch.link(nc.vector.reciprocal(RS[:], SD[:]))
                        if last_norm:
                            dve.wait_ge(turned, i * 2 + (k + 1))
                        for b in range(2):
                            dst = TT[:, b, :] if affine and not last_norm else XN[:, k, b, :]
                            ins = nc.vector.tensor_scalar(dst, src[b], MV[:, b, 0:1], RS[:, b:b + 1], ALU.subtract, ALU.mult)
                        if not last_norm or affine:
                            ch.link(ins)
                        else:
                            ins.then_inc(normed, 1)
                    if affine:
                        ga, bt = (v[:].rearrange("p (a d) -> p a d", a=1).broadcast_to([P, 2, DM]) for v in (GA, BT))
                        ch.link(nc.vector.tensor_tensor(TT[:], XN[:, k], ga, ALU.mult))
                        ch.link(nc.vector.tensor_tensor(XN[:, k], TT[:], bt, ALU.add))
                        dve.sem_inc(normed, 1)
                assert ch.n == links


def gate(nc, tally, tag, wg, bg, b2, ident, iota8, Y, XT, WD):
    with ExitStack() as ctx:
        sb, ps, sem = spaces(nc, ctx, tag)
        WG = sb("WG", [P, KC, E], F32)
        BG = sb("BG", [P, E], F32)
        B2 = sb("B2", [E, DM], F32)
        LG = sb("LG", [P, NT, E], F32)
        MX = sb("MX", [P, NT, 8], F32)
        IX = sb("IX", [P, NT, 8], U32)
        IF = sb("IF", [P, NT, 2], F32)
        DF = sb("DF", [P, NT, 1], F32)
        EE = sb("EE", [P, NT, 1], F32)
        SM = sb("SM", [P, NT, 1], F32)
        W12 = sb("W12", [P, NT, 2], F32)
        OH = sb("OH", [P, NT, 2, E], F32)
        WB = sb("WB", [P, NT, E], F32)
        WT = sb("WT", [E, NT, P], F32)
        pl = ps("pl", [P, 512], F32)
        pw = ps("pw", [E, 4, 4, P], F32)
        pb = ps("pb", [P, 3, 2, DM], F32)
        const_loaded, logits, chain, diff, ex, weighed, wd_turned, wd_copied, summed, added = (sem(n) for n in
            ("const_loaded", "logits", "chain", "diff", "ex", "weighed", "wd_turned", "wd_copied", "summed", "added"))
        block = ctx.enter_context(nc.Block())

        @block.sync
        def _(sp):
            sp.dma_start(WG[:], wg.rearrange("(c p) e -> p c e", p=P)).then_inc(const_loaded, 16)
            sp.dma_start(BG[:], bg.rearrange("(a e) -> a e", a=1).broadcast_to([P, E])).then_inc(const_loaded, 16)
            sp.dma_start(B2[:], b2).then_inc(const_loaded, 16)

        @block.tensor
        def _(pe):
            pe.wait_ge(const_loaded, 48)
            for n in range(NT):
                for c in range(KC):
                    last = nc.tensor.matmul(pl[:, n * E:(n + 1) * E], XT[:, c, n, :], WG[:, c, :], start=c == 0, stop=c == KC - 1)
            last.then_inc(logits, 1)
            pe.wait_ge(weighed, 1)
            for half in range(2):
                pe.wait_ge(wd_copied, half) if half else None
                for n in range(16):
                    last = nc.tensor.transpose(pw[:, n // 4, n % 4, :], WB[:, 16 * half + n, :], ident[:])
                last.then_inc(wd_turned, 1)
            pe.wait_ge(wd_copied, 2)
            for t in range(T):
                if t >= 3:
                    pe.wait_ge(added, t - 2)
                for b in range(2):
                    last = nc.tensor.matmul(pb[:, t % 3, b, :], WT[:, 2 * t + b, :], B2[:], start=True, stop=True)
                last.then_inc(summed, 1)

        @block.scalar
        def _(act):
            act.wait_ge(diff, 1)
            nc.scalar.activation(EE[:], DF[:], ACT.Exp).then_inc(ex, 1)
            for half in range(2):
                act.wait_ge(wd_turned, half + 1)
                nc.scalar.copy(WT[:, 16 * half:16 * half + 16, :].rearrange("e (a n) m -> e a n m", a=4), pw[:]).then_inc(wd_copied, 1)

        @block.vector
        def _(dve):
            ch = Chain(dve, chain)
            dve.wait_ge(const_loaded, 48)
            dve.wait_ge(logits, 1)
            ch.link(nc.vector.tensor_tensor(LG[:], pl[:, 0:NT * E].rearrange("p (n e) -> p n e", e=E),
                                            BG[:].rearrange("p (a e) -> p a e", a=1).broadcast_to([P, NT, E]), ALU.add))
            for n in range(NT):
                ins = nc.vector.max(MX[:, n, :], LG[:, n, :])
            ch.link(ins)
            for n in range(NT):
                ins = nc.vector.max_index(IX[:, n, :], MX[:, n, :], LG[:, n, :])
            ch.link(ins)
            nc.vector.tensor_copy(IF[:], IX[:, :, 0:2])
            nc.vector.tensor_tensor(DF[:], MX[:, :, 1:2], MX[:, :, 0:1], ALU.subtract).then_inc(diff, 1)
            dve.wait_ge(ex, 1)
            ch.link(nc.vector.tensor_scalar(SM[:], EE[:], 1.0, None, ALU.add))
            ch.link(nc.vector.reciprocal(W12[:, :, 0:1], SM[:]))
            ch.link(nc.vector.tensor_tensor(W12[:, :, 1:2], EE[:], W12[:, :, 0:1], ALU.mult))
            iota_b = iota8[:].rearrange("p (a b e) -> p a b e", a=1, b=1).broadcast_to([P, NT, 2, E])
            ch.link(nc.vector.tensor_tensor(OH[:], iota_b, IF[:].rearrange("p n (k a) -> p n k a", a=1).broadcast_to([P, NT, 2, E]), ALU.is_equal))
            ch.link(nc.vector.tensor_tensor(OH[:], OH[:], W12[:].rearrange("p n (k a) -> p n k a", a=1).broadcast_to([P, NT, 2, E]), ALU.mult))
            nc.vector.tensor_tensor(WB[:], OH[:, :, 0, :], OH[:, :, 1, :], ALU.add).then_inc(weighed, 1)
            ch.link(nc.vector.tensor_tensor(WD[:].rearrange("p e n -> p n e"), OH[:, :, 0, :], OH[:, :, 1, :], ALU.add))
            for t in range(T):
                dve.wait_ge(summed, t + 1)
                nc.vector.tensor_tensor(Y[:, 2 * t:2 * t + 2, :], Y[:, 2 * t:2 * t + 2, :], pb[:, t % 3], ALU.add).then_inc(added, 1)


def experts(nc, tally, tag, HH, w1, b1, w2, Y, XT, WD, dst):
    HT = HH // P
    CH = 512
    NCH = N // CH
    with ExitStack() as ctx:
        sb, ps, sem = spaces(nc, ctx, tag)
        W1 = sb("W1", [P, 2, KC, HH], F32)
        W2 = sb("W2", [P, 2, HT, DM], F32)
        B1 = sb("B1", [P, 2, HT], F32)
        G = sb("G", [P, 2, HT, CH], F32)
        WC = sb("WC", [P, 2, NT], F32)
        p1 = ps("p1", [P, 4, CH], F32)
        p2 = ps("p2", [P, 2, 4, DM], F32)
        w_loaded = [sem(f"w_loaded{k}") for k in range(2)]
        up, gelued, down, added, stored = (sem(n) for n in ("up", "gelued", "down", "added", "stored"))
        block = ctx.enter_context(nc.Block())
        C_DOWN, C_GEL, C_ADD = 2 * NCH, 4, 2

        @block.sync
        def _(sp):
            with sp.Fori(0, E // 2) as i:
                for k in range(2):
                    wait_apart(sp, tally, down, i * (2 * NCH) + NCH * (k + 1))
                    e = bass.ds(i * 2 + k, 1)
                    sp.dma_start(W1[:, k], w1[e].rearrange("a (c p) h -> p (a c) h", p=P)).then_inc(w_loaded[k], 16)
                    sp.dma_start(W2[:, k], w2[e].rearrange("a (c p) d -> p (a c) d", p=P)).then_inc(w_loaded[k], 16)
                    sp.dma_start(B1[:, k], b1[e].rearrange("a (c p) -> p (a c)", p=P), allow_slow_non_contiguous=True).then_inc(w_loaded[k], 16)
            sp.wait_ge(added, C_ADD + E * NCH)
            for t in range(4):
                sp.dma_start(tokens(dst)[:, 4 * t:4 * t + 4], Y[:, 8 * t:8 * t + 8, :].rearrange("p (t b) d -> p t b d", b=2)).then_inc(stored, 16)
            sp.wait_ge(stored, 64)

        @block.tensor
        def _(pe):
            pe.sem_inc(down, C_DOWN)
            with pe.Fori(0, E // 2) as i:
                def w1_part(v):
                    k, c = divmod(v, NCH)
                    if c == 0:
                        pe.wait_ge(w_loaded[k], i * 48 + 48)
                    for h in range(HT):
                        m = v * HT + h
                        pe.wait_ge(gelued, i * (2 * NCH * HT) + (m + 1))
                        for kc in range(KC):
                            last = nc.tensor.matmul(p1[:, m % 4, :], W1[:, k, kc, h * P:(h + 1) * P],
                                                    XT[:, kc, 4 * c:4 * c + 4, :].rearrange("p n m -> p (n m)"),
                                                    start=kc == 0, stop=kc == KC - 1)
                        last.then_inc(up, 1)

                def w2_part(v):
                    k, c = divmod(v, NCH)
                    pe.wait_ge(gelued, i * (2 * NCH * HT) + (C_GEL + (v + 1) * HT))
                    pe.wait_ge(added, i * (2 * NCH) + (v + 1))
                    for n in range(4):
                        for h in range(HT):
                            last = nc.tensor.matmul(p2[:, v % 2, n, :], G[:, v % 2, h, n * P:(n + 1) * P], W2[:, k, h, :],
                                                    start=h == 0, stop=h == HT - 1)
                    last.then_inc(down, 1)

                w1_part(0)
                for v in range(1, 2 * NCH):
                    w1_part(v)
                    w2_part(v - 1)
                w2_part(2 * NCH - 1)

        @block.scalar
        def _(act):
            act.sem_inc(gelued, C_GEL)
            with act.Fori(0, E // 2) as i:
                for v in range(2 * NCH):
                    k = v // NCH
                    act.wait_ge(down, i * (2 * NCH) + (C_DOWN + v - 1))
                    if v % NCH == 0:
                        act.wait_ge(w_loaded[k], i * 48 + 48)
                    for h in range(HT):
                        m = v * HT + h
                        act.wait_ge(up, i * (2 * NCH * HT) + (m + 1))
                        nc.scalar.activation(G[:, v % 2, h, :], p1[:, m % 4, :], ACT.Gelu, bias=B1[:, k, h:h + 1]).then_inc(gelued, 1)

        @block.vector
        def _(dve):
            dve.sem_inc(added, C_ADD)
            wc = sem("wc")
            with dve.Fori(0, E // 2) as i:
                for k in range(2):
                    dve.wait_ge(added, i * (2 * NCH) + (C_ADD - 2 + NCH * k + 1))
                    nc.vector.tensor_copy(WC[:, k, :], WD[:, bass.ds(i * 2 + k, 1), :].rearrange("p a n -> p (a n)")).then_inc(wc, 1)
                    dve.wait_ge(wc, i * 2 + (k + 1))
                    for c in range(NCH):
                        v = k * NCH + c
                        dve.wait_ge(down, i * (2 * NCH) + (C_DOWN + v + 1))
                        for n in range(4):
                            y = Y[:, 4 * c + n, :]
                            last = nc.vector.scalar_tensor_tensor(y, p2[:, v % 2, n, :], WC[:, k, 4 * c + n:4 * c + n + 1], y, ALU.mult, ALU.add)
                        last.then_inc(added, 1)


def program(nc, x, adj, L0_gnn_W, L0_gnn_a_src, L0_gnn_a_dst, L0_ffn_Wg, L0_ffn_bg, L0_ffn_W1, L0_ffn_b1, L0_ffn_W2, L0_ffn_b2,
            L1_gnn_W, L1_gnn_a_src, L1_gnn_a_dst, L1_gnn_bias, L1_ffn_gamma, L1_ffn_beta, L1_ffn_Wr, L1_ffn_br, L1_ffn_W1,
            L1_ffn_b1, L1_ffn_W2, L1_ffn_b2, out, stages=99):
    nc.disable_value_cache = True
    mask_t = nc.dram_tensor("mask_t", [P, T, 2 * N], U8).ap()
    x_mid = nc.dram_tensor("x_mid", [N, DM], F32).ap()
    layers = [
        dict(H=4, D=64, IB=512, x=x, dst=x_mid, w_rows=L0_gnn_W, w_cols=None, a=(L0_gnn_a_src, L0_gnn_a_dst), elu=True, bias=None,
             gamma=None, beta=None, wg=L0_ffn_Wg, bg=L0_ffn_bg, w1=L0_ffn_W1, b1=L0_ffn_b1, w2=L0_ffn_W2, b2=L0_ffn_b2, HH=1024),
        dict(H=8, D=32, IB=1024, x=x_mid, dst=out, w_rows=None, w_cols=L1_gnn_W, a=(L1_gnn_a_src, L1_gnn_a_dst), elu=False,
             bias=L1_gnn_bias, gamma=L1_ffn_gamma, beta=L1_ffn_beta, wg=L1_ffn_Wr, bg=L1_ffn_br, w1=L1_ffn_W1, b1=L1_ffn_b1,
             w2=L1_ffn_W2, b2=L1_ffn_b2, HH=512),
    ]
    with ExitStack() as top:
        sb0, _, sem0 = spaces(nc, top, "all")
        tally = sem0("tally")
        ident = sb0("ident", [P, P], F32)
        ident16 = sb0("ident16", [P, P], F16)
        eye = sb0("eye", [P, 4 * P], F8)
        iota8 = sb0("iota8", [P, E], F32)
        constants(nc, ident, ident16, eye, iota8)
        transpose_mask(nc, tally, adj, mask_t, ident16)
        for n, L in enumerate(layers):
            tag, H, D = f"L{n}", L["H"], L["D"]
            if n >= stages:
                break
            with ExitStack() as layer:
                sbl, _, _ = spaces(nc, layer, tag)
                OUT = sbl("OUT", [P, NT, DM], F32)
                with ExitStack() as att:
                    sba, _, _ = spaces(nc, att, tag)
                    UV = sba("UV", [P, H, NT, 4, D + 1], F16)
                    NEGD, BIGD, AL, BE = (sba(v, [P, NT, H], F32) for v in ("NEGD", "BIGD", "AL", "BE"))
                    s_rows = nc.dram_tensor(f"{tag}_s_rows", [H, N], F32).ap()
                    project(nc, tally, tag + "p", H, D, L["x"], L["w_rows"], L["w_cols"], *L["a"], ident, s_rows, UV, NEGD, BIGD, AL, BE)
                    if n == 1:
                        add_diagonal(nc, tally, mask_t, eye)
                    attention(nc, tally, tag + "a", H, D, L["IB"], s_rows, mask_t, UV, NEGD, BIGD, AL, BE, OUT)
                Y = sbl("Y", [P, NT, DM], F32)
                XT = sbl("XT", [P, KC, NT, P], F32)
                WD = sbl("WD", [P, E, NT], F32)
                residual_norm(nc, tally, tag + "r", L["x"], OUT, L["elu"], L["bias"], L["gamma"], L["beta"], ident, Y, XT)
                gate(nc, tally, tag + "g", L["wg"], L["bg"], L["b2"], ident, iota8, Y, XT, WD)
                experts(nc, tally, tag + "e", L["HH"], L["w1"], L["b1"], L["w2"], Y, XT, WD, L["dst"] if stages > n + 1 else out)


_INS = ["x", "adj", "L0_gnn_W", "L0_gnn_a_src", "L0_gnn_a_dst", "L0_ffn_Wg", "L0_ffn_bg", "L0_ffn_W1", "L0_ffn_b1", "L0_ffn_W2",
        "L0_ffn_b2", "L1_gnn_W", "L1_gnn_a_src", "L1_gnn_a_dst", "L1_gnn_bias", "L1_ffn_gamma", "L1_ffn_beta", "L1_ffn_Wr",
        "L1_ffn_br", "L1_ffn_W1", "L1_ffn_b1", "L1_ffn_W2", "L1_ffn_b2"]


def kernel(**inputs):
    from concourse import bacc
    from concourse.bass_utils import run_bass_kernel_spmd

    nc = bacc.Bacc("TRN2", target_bir_lowering=False, num_devices=1)
    arrays, args = {}, {}
    for name in _INS:
        a = np.ascontiguousarray(inputs[name])
        arrays[f"in_{name}"] = a
        args[name] = nc.dram_tensor(f"in_{name}", a.shape, mybir.dt.from_np(a.dtype), kind="ExternalInput").ap()
    out = nc.dram_tensor("out", [N, DM], F32, kind="ExternalOutput").ap()
    program(nc, out=out, **args)
    r = run_bass_kernel_spmd(nc, [arrays], core_ids=[0])
    return r.results[0]["out"]
```

```python
from contextlib import ExitStack

import concourse.bass as bass
import numpy as np
from concourse import mybir

F32, F16, F8 = mybir.dt.float32, mybir.dt.float16, mybir.dt.float8e4
U8, U32 = mybir.dt.uint8, mybir.dt.uint32
ALU = mybir.AluOpType
ACT = mybir.ActivationFunctionType
X = mybir.AxisListType.X

P = 128
N = 4096
DM = 256
T = N // (2 * P)
NT = 2 * T
KC = DM // P
E = 8
TILES = (2 * N + E * (P - 1)) // P
TILES += TILES % 2
EPS = 1e-5
MASK_SHIFT = 5
STEEP = 2.0 ** 60
TOP = 2.0 ** 14


class Chain:

    def __init__(self, eng, sem, base=0):
        self.eng, self.sem, self.base, self.n = eng, sem, base, 0

    def link(self, ins, tally=None):
        self.n += 1
        ins.then_inc(self.sem, 1)
        if tally is not None:
            wait_apart(self.eng, tally, self.sem, self.base + self.n)
        else:
            self.eng.wait_ge(self.sem, self.base + self.n)


def wait_apart(eng, tally, sem, value):
    eng.wait_ge(sem, value)
    eng.sem_inc(tally, 1)


def spaces(nc, ctx, tag):
    def sb(name, shape, dt):
        return ctx.enter_context(nc.sbuf_tensor(f"{tag}_{name}", shape, dt))

    def ps(name, shape, dt):
        return ctx.enter_context(nc.psum_tensor(f"{tag}_{name}", shape, dt))

    held = []

    def sem(name):
        held.append(nc.alloc_semaphore(f"{tag}_{name}"))
        return held[-1]

    def clear():
        if held:
            nc.clear_and_free_semaphores(held)
            nc.all_engine_barrier()

    ctx.callback(clear)
    return sb, ps, sem


def tokens(x):
    return x.rearrange("(t p b) d -> p t b d", p=P, b=2)


def constants(nc, ident, ident16, eye, iota8, tri, ones, firsts, slots):
    with ExitStack() as ctx:
        sb, _, sem = spaces(nc, ctx, "const")
        eye32 = sb("eye32", [P, 4 * P], F32)
        made = sem("made")
        block = ctx.enter_context(nc.Block())

        @block.gpsimd
        def _(pool):
            nc.gpsimd.memset(ident[:], 0.0).then_inc(made, 1)
            nc.gpsimd.memset(ident16[:], 0.0).then_inc(made, 1)
            nc.gpsimd.memset(eye32[:], 0.0).then_inc(made, 1)
            nc.gpsimd.iota(iota8[:], pattern=[[1, E]], base=0, channel_multiplier=0,
                           allow_small_or_imprecise_dtypes=True).then_inc(made, 1)
            nc.gpsimd.iota(firsts[:], pattern=[[P, NT]], base=0, channel_multiplier=0, allow_small_or_imprecise_dtypes=True).then_inc(made, 1)
            nc.gpsimd.iota(slots[:], pattern=[[1, TILES]], base=0, channel_multiplier=0, allow_small_or_imprecise_dtypes=True).then_inc(made, 1)
            nc.gpsimd.memset(tri[:], 0.0).then_inc(made, 1)
            nc.gpsimd.memset(ones[:], 1.0).then_inc(made, 1)
            pool.wait_ge(made, 8)
            nc.gpsimd.affine_select(out=tri[:], in_=tri[:], compare_op=ALU.is_ge, fill=1.0, base=0,
                                    pattern=[[-1, P]], channel_multiplier=1).then_inc(made, 1)
            for m in (ident, ident16):
                nc.gpsimd.affine_select(out=m[:], in_=m[:], compare_op=ALU.not_equal, fill=1.0, base=0,
                                        pattern=[[-1, P]], channel_multiplier=1).then_inc(made, 1)
            ev = eye32[:].rearrange("p (i b) -> p i b", b=2)
            nc.gpsimd.affine_select(out=ev, in_=ev, compare_op=ALU.not_equal, fill=0.125, base=0,
                                    pattern=[[-1, 2 * P], [1, 2]], channel_multiplier=2).then_inc(made, 1)
            pool.wait_ge(made, 12)
            nc.gpsimd.tensor_copy(eye[:], eye32[:], saturate=False).then_inc(made, 1)
            pool.wait_ge(made, 13)


def transpose_mask(nc, tally, adj, mask_t, ident16):
    G, A = 8, 4
    adj_v = adj.rearrange("(g a q) j -> g a q j", a=A, q=P)
    with ExitStack() as ctx:
        sb, ps, sem = spaces(nc, ctx, "mask")
        rows = sb("rows", [P, A, N], U8)
        blk = sb("blk", [P, 2, T, 2 * A * P], U8)
        pt = ps("pt", [P, 2, T, P], F16)
        rows_loaded = [sem(f"rows_loaded{a}") for a in range(A)]
        transposed = sem("transposed")
        shifted = sem("shifted")
        stored = [sem(f"stored{k}") for k in range(2)]
        block = ctx.enter_context(nc.Block())

        @block.sync
        def _(sp):
            with sp.Fori(0, G) as g:
                for a in range(A):
                    wait_apart(sp, tally, transposed, g * A + (a + 1))
                    sp.dma_start(rows[:, a, :], adj_v[bass.ds(g, 1), a]).then_inc(rows_loaded[a], 16)

        @block.tensor
        def _(pe):
            pe.sem_inc(transposed, A)
            with pe.Fori(0, G) as g:
                for a in range(A):
                    pe.wait_ge(rows_loaded[a], g * 16 + 16)
                    pe.wait_ge(shifted, g * A + (a + 1))
                    pairs = rows[:, a, :].bitcast(F16)
                    for t in range(T):
                        last = nc.tensor.transpose(pt[:, a % 2, t, :], pairs[:, t * P:(t + 1) * P], ident16[:])
                    last.then_inc(transposed, 1)

        @block.vector
        def _(dve):
            dve.sem_inc(shifted, 2)
            with dve.Fori(0, G // 2) as g2:
                for k in range(2):
                    for a in range(A):
                        dve.wait_ge(transposed, g2 * 2 * A + (A + k * A + a + 1))
                        if a == 0:
                            dve.wait_ge(stored[k], g2 * 16 + 16)
                        nc.vector.tensor_scalar(
                            blk[:, k, :, 2 * P * a:2 * P * (a + 1)].bitcast(U32), pt[:, a % 2].bitcast(U32),
                            MASK_SHIFT, None, ALU.logical_shift_left).then_inc(shifted, 1)

        @block.scalar
        def _(act):
            act.sem_inc(stored[0], 16)
            act.sem_inc(stored[1], 16)
            with act.Fori(0, G // 2) as g2:
                for k in range(2):
                    act.wait_ge(shifted, g2 * 2 * A + (2 + (k + 1) * A))
                    width = 2 * A * P
                    act.dma_start(mask_t[:, :, bass.ds(g2 * 2 * width + k * width, width)], blk[:, k]).then_inc(stored[k], 16)
            for k in range(2):
                act.wait_ge(stored[k], 16 + 16 * (G // 2))


def add_diagonal(nc, tally, mask_t, eye):
    with ExitStack() as ctx:
        sb, _, sem = spaces(nc, ctx, "diag")
        W = 4 * P
        d = sb("d", [P, T, W], U8)
        loaded, ored, stored = sem("loaded"), sem("ored"), sem("stored")
        block = ctx.enter_context(nc.Block())

        @block.sync
        def _(sp):
            for t in range(T):
                sp.dma_start(d[:, t, :], mask_t[:, t, t * W:(t + 1) * W]).then_inc(loaded, 16)
            sp.wait_ge(ored, 1)
            for t in range(T):
                sp.dma_start(mask_t[:, t, t * W:(t + 1) * W], d[:, t, :]).then_inc(stored, 16)
            sp.wait_ge(stored, 16 * T)

        @block.vector
        def _(dve):
            dve.wait_ge(loaded, 16 * T)
            e = eye[:].bitcast(U32)
            nc.vector.tensor_tensor(d[:].bitcast(U32), d[:].bitcast(U32),
                                    e.rearrange("p (a w) -> p a w", a=1).broadcast_to([P, T, W // 4]),
                                    ALU.bitwise_or).then_inc(ored, 1)


def project(nc, tally, tag, H, D, x, w_rows, w_cols, a_src, a_dst, ident, s_rows, UV, NEGD, BIGD, AL, BE):
    D1 = D + 1
    C = DM + 2 * H
    xv = tokens(x)
    with ExitStack() as ctx:
        sb, ps, sem = spaces(nc, ctx, tag)
        WR = sb("WR", [P, KC, DM], F32)
        WC = sb("WC", [P, KC, C], F32)
        AB = sb("AB", [P, KC, 2 * H], F32)
        XS = sb("XS", [P, 2, 2, DM], F32)
        XN = sb("XN", [P, 2, 2, DM], F32)
        XT = sb("XT", [P, 2, KC, 2, P], F32)
        ST = sb("ST", [P, 2, 2, 6], F32)
        MV = sb("MV", [P, 2, 2, 2], F32)
        SD = sb("SDEV", [P, 2, 2], F32)
        RS = sb("RS", [P, 2, 2], F32)
        HB = sb("HB", [P, NT, DM], F32)
        SC = sb("SC", [P, NT, 2 * H], F32)
        SR = sb("SR", [H, N], F32)
        MX = sb("MX", [P, H + 1], F32)
        MA = sb("MA", [P, H + 1], F32)
        KA = sb("KA", [P, 3], F32)
        EPT = sb("EPT", [P, 1], F32)
        Z = sb("Z", [P, 4, NT, H], F32)
        EX = sb("EX", [P, 2, NT, H], F32)
        TM = sb("TM", [P, 2, NT, D1], F32)
        pt = ps("pt", [P, 2, 4, P], F32)
        ph = ps("ph", [P, 2, 2, 512], F32)
        pr = ps("pr", [P, 2, 512], F32)
        w_loaded, zeroed, w_turned, w_copied, folded, w_ready = (sem(n) for n in
            ("w_loaded", "zeroed", "w_turned", "w_copied", "folded", "w_ready"))
        x_loaded = [sem(f"x_loaded{k}") for k in range(2)]
        stats, std, normed, turned, xt_ready, projected, h_out, row_out, dve_chain = (sem(n) for n in
            ("stats", "std", "normed", "turned", "xt_ready", "projected", "h_out", "row_out", "dve_chain"))
        maxes, all_max, args, exps, scaled, hi_done, rows_stored = (sem(n) for n in
            ("maxes", "all_max", "args", "exps", "scaled", "hi_done", "rows_stored"))
        block = ctx.enter_context(nc.Block())
        by_rows = w_rows is not None
        n_w = KC + 2 * H

        @block.sync
        def _(sp):
            for c in range(KC):
                if by_rows:
                    sp.dma_start(WR[:, c, :], w_rows[c * P:(c + 1) * P, :]).then_inc(w_loaded, 16)
                else:
                    sp.dma_start(WC[:, c, 0:DM].rearrange("p (h f) -> p h f", h=H),
                                 w_cols[:, c * P:(c + 1) * P, :].rearrange("h p f -> p h f")).then_inc(w_loaded, 16)
            sp.wait_ge(zeroed, 1)
            for k, a in enumerate((a_src, a_dst)):
                for h in range(H):
                    c, r = divmod(h * D, P)
                    sp.dma_start(AB[r:r + D, c, k * H + h:k * H + h + 1], a[h:h + 1, :].rearrange("a d -> d a")).then_inc(w_loaded, 16)
            with sp.Fori(0, T // 2) as i:
                for k in range(2):
                    wait_apart(sp, tally, normed, i * 2 + (k + 1))
                    sp.dma_start(XS[:, k], xv[:, bass.ds(i * 2 + k, 1)]).then_inc(x_loaded[k], 16)
            sp.wait_ge(row_out, 2 + T)
            sp.dma_start(s_rows, SR[:]).then_inc(rows_stored, 16)
            sp.wait_ge(rows_stored, 16)

        @block.gpsimd
        def _(pool):
            nc.gpsimd.memset(AB[:], 0.0).then_inc(zeroed, 1)
            pool.wait_ge(maxes, 1)
            nc.gpsimd.partition_all_reduce(MA[:], MX[:], P, bass.bass_isa.ReduceOp.max).then_inc(all_max, 1)

        @block.tensor
        def _(pe):
            pe.sem_inc(turned, 2)
            pe.sem_inc(projected, 2)
            pe.wait_ge(w_loaded, 16 * n_w)
            for c in range(KC):
                for c2 in range(KC):
                    src = WR[:, c, c2 * P:(c2 + 1) * P] if by_rows else WC[:, c, c2 * P:(c2 + 1) * P]
                    last = nc.tensor.transpose(pt[:, c, c2, :], src, ident[:])
            last.then_inc(w_turned, 1)
            pe.wait_ge(w_copied, 1)
            for c in range(KC):
                for c2 in range(KC):
                    last = nc.tensor.matmul(pr[:, c, 0:2 * H], WR[:, c2, c * P:(c + 1) * P], AB[:, c2, :],
                                            start=c2 == 0, stop=c2 == KC - 1)
            last.then_inc(folded, 1)
            pe.wait_ge(w_ready, 1)
            with pe.Fori(0, T // 2) as i:
                for k in range(2):
                    pe.wait_ge(normed, i * 2 + (2 + k + 1))
                    pe.wait_ge(xt_ready, i * 2 + (k + 1))
                    for c in range(KC):
                        for b in range(2):
                            last = nc.tensor.transpose(pt[:, k, 2 * c + b, :], XN[:, k, b, c * P:(c + 1) * P], ident[:])
                    last.then_inc(turned, 1)
                for k in range(2):
                    pe.wait_ge(xt_ready, i * 2 + (2 + k + 1))
                    pe.wait_ge(h_out, i * 2 + (k + 1))
                    pe.wait_ge(row_out, i * 2 + (k + 1))
                    for b in range(2):
                        for c in range(KC):
                            nc.tensor.matmul(ph[:, k, b, 0:C], XT[:, k, c, b, :], WC[:, c, :], start=c == 0, stop=c == KC - 1)
                    for c in range(KC):
                        last = nc.tensor.matmul(pr[0:H, k, 0:2 * P], WC[:, c, DM:DM + H],
                                                XT[:, k, c].rearrange("p b m -> p (b m)"), start=c == 0, stop=c == KC - 1)
                    last.then_inc(projected, 1)

        @block.scalar
        def _(act):
            act.sem_inc(xt_ready, 2)
            act.sem_inc(row_out, 2)
            act.wait_ge(w_turned, 1)
            for c in range(KC):
                for c2 in range(KC):
                    dst = WC[:, c2, c * P:(c + 1) * P] if by_rows else WR[:, c2, c * P:(c + 1) * P]
                    last = nc.scalar.copy(dst, pt[:, c, c2, :])
            last.then_inc(w_copied, 1)
            act.wait_ge(folded, 1)
            nc.scalar.copy(WC[:, :, DM:C], pr[:, :, 0:2 * H]).then_inc(w_ready, 1)
            with act.Fori(0, T // 2) as i:
                for k in range(2):
                    act.wait_ge(stats, i * 2 + (k + 1))
                    nc.scalar.activation(SD[:, k, :], MV[:, k, :, 1], ACT.Sqrt, bias=EPT[:, 0:1]).then_inc(std, 1)
                for k in range(2):
                    act.wait_ge(turned, i * 2 + (2 + k + 1))
                    act.wait_ge(projected, i * 2 + (k + 1))
                    nc.scalar.copy(XT[:, k].rearrange("p c b m -> p (c b) m"), pt[:, k]).then_inc(xt_ready, 1)
                for k in range(2):
                    act.wait_ge(projected, i * 2 + (2 + k + 1))
                    nc.scalar.copy(SR[:, bass.ds(i * 4 * P + k * 2 * P, 2 * P)].rearrange("h (m b) -> h b m", b=2),
                                   pr[0:H, k, 0:2 * P].rearrange("h (b m) -> h b m", b=2)).then_inc(row_out, 1)
            act.wait_ge(args, 1)
            nc.scalar.activation(EX[:, 0], Z[:, 1], ACT.Exp)
            nc.scalar.activation(EX[:, 1], Z[:, 1], ACT.Exp, scale=0.2)
            nc.scalar.activation(AL[:], Z[:, 2], ACT.Exp)
            nc.scalar.activation(BE[:], Z[:, 3], ACT.Exp).then_inc(exps, 1)
            for n in range(2 * H):
                h, g = divmod(n, 2)
                act.wait_ge(scaled, n + 1)
                nc.scalar.copy(UV[:, h, :, 2 * g, :], TM[:, n % 2]).then_inc(hi_done, 1)

        @block.vector
        def _(dve):
            dve.sem_inc(normed, 2)
            dve.sem_inc(h_out, 2)
            nc.vector.memset(EPT[:], EPS).then_inc(dve_chain, 1)
            dve.wait_ge(dve_chain, 1)
            links = 6
            with dve.Fori(0, T // 2) as i:
                ch = Chain(dve, dve_chain, dve.snap(i * links + 1))
                for k in range(2):
                    dve.wait_ge(x_loaded[k], i * 16 + 16)
                    nc.vector.bn_stats(ST[:, k, 0, :], XS[:, k, 0, :])
                    ch.link(nc.vector.bn_stats(ST[:, k, 1, :], XS[:, k, 1, :]), tally=tally)
                    nc.vector.bn_aggr(MV[:, k, 0, :], ST[:, k, 0, :])
                    nc.vector.bn_aggr(MV[:, k, 1, :], ST[:, k, 1, :]).then_inc(stats, 1)
                for k in range(2):
                    dve.wait_ge(std, i * 2 + (k + 1))
                    ch.link(nc.vector.reciprocal(RS[:, k, :], SD[:, k, :]))
                    dve.wait_ge(turned, i * 2 + (k + 1))
                    ch.link(nc.vector.tensor_scalar(XN[:, k, 0, :], XS[:, k, 0, :], MV[:, k, 0, 0:1], RS[:, k, 0:1], ALU.subtract, ALU.mult))
                    nc.vector.tensor_scalar(XN[:, k, 1, :], XS[:, k, 1, :], MV[:, k, 1, 0:1], RS[:, k, 1:2],
                                            ALU.subtract, ALU.mult).then_inc(normed, 1)
                for k in range(2):
                    dve.wait_ge(projected, i * 2 + (2 + k + 1))
                    nc.vector.tensor_copy(HB[:, bass.ds(i * 4 + 2 * k, 2), :], ph[:, k, :, 0:DM])
                    nc.vector.tensor_copy(SC[:, bass.ds(i * 4 + 2 * k, 2), :], ph[:, k, :, DM:C]).then_inc(h_out, 1)
                assert ch.n == links
            ch = Chain(dve, dve_chain, 1 + links * (T // 2))
            dve.wait_ge(h_out, 2 + T)
            nc.vector.tensor_reduce(MX[:, 0:H], SC[:, :, H:2 * H].rearrange("p n h -> p h n"), X, ALU.max)
            nc.vector.tensor_reduce(MX[:, H:H + 1], HB[:].rearrange("p n d -> p (n d)"), X, ALU.max,
                                    apply_absolute_value=True).then_inc(maxes, 1)
            nc.vector.tensor_scalar(NEGD[:], SC[:, :, H:2 * H], -1.0, None, ALU.mult)
            nc.vector.tensor_scalar(BIGD[:], SC[:, :, H:2 * H], STEEP, None, ALU.mult)
            dve.wait_ge(all_max, 1)
            dmax = MA[:, 0:H].rearrange("p (a h) -> p a h", a=1).broadcast_to([P, NT, H])
            nc.vector.tensor_tensor(Z[:, 1], SC[:, :, H:2 * H], dmax, ALU.subtract)
            ch.link(nc.vector.tensor_tensor(Z[:, 0], SC[:, :, 0:H], dmax, ALU.add))
            nc.vector.tensor_scalar(Z[:, 2], Z[:, 0], 0.8, 0.0, ALU.mult, ALU.min)
            ch.link(nc.vector.tensor_scalar(Z[:, 3], Z[:, 0], -0.8, 0.0, ALU.mult, ALU.min))
            dve.sem_inc(args, 1)
            ch.link(nc.vector.tensor_scalar(KA[:, 0:1], MA[:, H:H + 1], 1.0, None, ALU.max))
            ch.link(nc.vector.reciprocal(KA[:, 1:2], KA[:, 0:1]))
            ch.link(nc.vector.tensor_scalar(KA[:, 2:3], KA[:, 1:2], TOP, None, ALU.mult))
            dve.wait_ge(exps, 1)
            ch.link(nc.vector.tensor_scalar(EX[:], EX[:], KA[:, 2:3], None, ALU.mult))

            def scale(n):
                h, g = divmod(n, 2)
                if n >= 2:
                    dve.wait_ge(hi_done, n - 1)
                e = EX[:, g, :, h:h + 1]
                nc.vector.tensor_copy(TM[:, n % 2, :, D:D1], e)
                nc.vector.tensor_tensor(TM[:, n % 2, :, 0:D], HB[:, :, h * D:(h + 1) * D], e.broadcast_to([P, NT, D]),
                                        ALU.mult).then_inc(scaled, 1)

            def low(n):
                h, g = divmod(n, 2)
                dve.wait_ge(hi_done, n + 1)
                dve.wait_ge(scaled, n + 1)
                ch.link(nc.vector.tensor_tensor(UV[:, h, :, 2 * g + 1, :], TM[:, n % 2], UV[:, h, :, 2 * g, :], ALU.subtract))

            scale(0)
            for n in range(1, 2 * H):
                scale(n)
                low(n - 1)
            low(2 * H - 1)


def attention(nc, tally, tag, H, D, IB, s_rows, mask_t, UV, NEGD, BIGD, AL, BE, OUT):
    D1 = D + 1
    W = 2 * D1
    NI = IB // P
    NB = N // IB
    PER = NI // 4
    U = 16
    NS, NM, NSB = 4, 4, 4
    with ExitStack() as ctx:
        sb, ps, sem = spaces(nc, ctx, tag)
        MB = sb("MB", [P, T, 2 * IB], U8)
        SB = sb("SB", [P, NSB, IB], F32)
        SS = sb("SS", [P, NS, 2 * IB], U8)
        M1 = sb("M1", [P, NM, 2 * IB], U8)
        OE = sb("OE", [P, 2, NI, 3, 2, D1], F32)
        R = sb("R", [P, NI, 3, D1], F32)
        TA = sb("TA", [P, NI, D1], F32)
        TB = sb("TB", [P, NI, D1], F32)
        TC = sb("TC", [P, NI, D1], F32)
        po = ps("po", [P, 2, 4, 512], F32)
        mask_loaded = [sem(f"mask_loaded{g}") for g in range(4)]
        s_loaded = [sem(f"s_loaded{k}") for k in range(NSB)]
        stepped_act, stepped_dve, summed, masked, evacuated, combined, chain = (sem(n) for n in
            ("stepped_act", "stepped_dve", "summed", "masked", "evacuated", "combined", "chain"))
        C_SUM, C_MASKED, C_EV, C_COMB = U * H, U * NSB, 2, 2
        block = ctx.enter_context(nc.Block())

        @block.sync
        def _(sp):
            with sp.Fori(0, NB) as ib:
                iu = sp.snap(ib * (U * H))
                def rows(h):
                    wait_apart(sp, tally, masked, iu + U * (h + 1))
                    sp.dma_start(SB[:, h % NSB, :], s_rows[h:h + 1, bass.ds(ib * IB, IB)].broadcast_to([P, IB])).then_inc(s_loaded[h % NSB], 16)

                for h in range(NSB - 1):
                    rows(h)
                for g in range(4):
                    wait_apart(sp, tally, summed, iu + (U * (H - 1) + 4 * (g + 1)))
                    sp.dma_start(MB[:, 4 * g:4 * g + 4, :], mask_t[:, 4 * g:4 * g + 4, bass.ds(ib * 2 * IB, 2 * IB)]).then_inc(mask_loaded[g], 16)
                for h in range(NSB - 1, H):
                    rows(h)

        @block.scalar
        def _(act):
            act.sem_inc(evacuated, C_EV)
            with act.Fori(0, NB) as ib:
                iu, ih, isl = act.snap(ib * (U * H)), act.snap(ib * H), act.snap(ib * (16 * H // NSB))
                def evacuate(h):
                    act.wait_ge(summed, iu + (C_SUM + U * (h + 1)))
                    act.wait_ge(combined, ih + (h + 1))
                    nc.scalar.copy(OE[:, h % 2].rearrange("p (a n) g l d -> p a (n g l d)", n=PER),
                                   po[:, h % 2, :, 0:PER * 3 * W]).then_inc(evacuated, 1)

                for h in range(H):
                    act.wait_ge(s_loaded[h % NSB], isl + 16 * (h // NSB + 1))
                    for t in range(T):
                        u = U * h + t
                        wait_apart(act, tally, masked, iu + (C_MASKED + u - NS + 1))
                        nc.scalar.activation(SS[:, u % NS, :].bitcast(F8).rearrange("p (i b) -> p b i", b=2)[:, 0, :], SB[:, h % NSB, :],
                                             ACT.Sigmoid, bias=BIGD[:, 2 * t, h:h + 1], scale=STEEP, saturate=False).then_inc(stepped_act, 1)
                        if t == 4 and h > 0:
                            evacuate(h - 1)
                evacuate(H - 1)

        @block.vector
        def _(dve):
            dve.sem_inc(masked, C_MASKED)
            dve.sem_inc(combined, C_COMB)
            links = 6 * H
            with dve.Fori(0, NB) as ib:
                iu, ih, isl, it = dve.snap(ib * (U * H)), dve.snap(ib * H), dve.snap(ib * (16 * H // NSB)), dve.snap(ib * NI)
                ch = Chain(dve, chain, dve.snap(ib * links))

                def step(u):
                    h, t = divmod(u, U)
                    if t == 0:
                        dve.wait_ge(s_loaded[h % NSB], isl + 16 * (h // NSB + 1))
                    dve.wait_ge(masked, iu + (C_MASKED + u - NS + 1))
                    nc.vector.tensor_scalar(SS[:, u % NS, :].rearrange("p (i b) -> p b i", b=2)[:, 1, :], SB[:, h % NSB, :],
                                            NEGD[:, 2 * t + 1, h:h + 1], float(1 << MASK_SHIFT), ALU.is_gt, ALU.mult).then_inc(stepped_dve, 1)

                def mask(u):
                    h, t = divmod(u, U)
                    dve.wait_ge(stepped_dve, iu + (u + 1))
                    dve.wait_ge(stepped_act, iu + (u + 1))
                    dve.wait_ge(summed, iu + (C_SUM + u - NM + 1))
                    if h == 0 and t % 4 == 0:
                        dve.wait_ge(mask_loaded[t // 4], ib * 16 + 16)
                    nc.vector.tensor_tensor(M1[:, u % NM, :].bitcast(U32), SS[:, u % NS, :].bitcast(U32), MB[:, t, :].bitcast(U32),
                                            ALU.bitwise_and).then_inc(masked, 1)

                def combine(h):
                    dve.wait_ge(evacuated, ih + (C_EV + h + 1))
                    al = AL[:, bass.ds(it, NI), h:h + 1].broadcast_to([P, NI, D1])
                    be = BE[:, bass.ds(it, NI), h:h + 1].broadcast_to([P, NI, D1])
                    ch.link(nc.vector.tensor_tensor(R[:], OE[:, h % 2, :, :, 0, :], OE[:, h % 2, :, :, 1, :], ALU.add))
                    dve.sem_inc(combined, 1)
                    ch.link(nc.vector.tensor_tensor(TB[:], R[:, :, 2, :], R[:, :, 1, :], ALU.subtract))
                    nc.vector.tensor_tensor(TA[:], R[:, :, 0, :], al, ALU.mult)
                    ch.link(nc.vector.tensor_tensor(TC[:], TB[:], be, ALU.mult))
                    ch.link(nc.vector.tensor_tensor(TB[:], TA[:], TC[:], ALU.add))
                    ch.link(nc.vector.reciprocal(TA[:, :, 0:1], TB[:, :, D:D1]))
                    ch.link(nc.vector.tensor_tensor(OUT[:, bass.ds(it, NI), h * D:(h + 1) * D], TB[:, :, 0:D],
                                                    TA[:, :, 0:1].broadcast_to([P, NI, D]), ALU.mult))

                step(0)
                for u in range(U * H):
                    if u + 1 < U * H:
                        step(u + 1)
                    mask(u)
                    if u % U == 8 and u > U:
                        combine(u // U - 1)
                combine(H - 1)
                assert ch.n == links

        @block.tensor
        def _(pe):
            pe.sem_inc(summed, C_SUM)
            m1 = M1[:].bitcast(F8).rearrange("p s (q m bi bj) -> p s q bi bj m", bi=2, bj=2, m=P)
            mb = MB[:].bitcast(F8).rearrange("p t (q m bi bj) -> p t q bi bj m", bi=2, bj=2, m=P)
            with pe.Fori(0, NB) as ib:
                iu, ih = pe.snap(ib * (U * H)), pe.snap(ib * H)
                for h in range(H):
                    pe.wait_ge(evacuated, ih + (h + 1))
                    for t in range(T):
                        u = U * h + t
                        wait_apart(pe, tally, masked, iu + (C_MASKED + u + 1))
                        for bj in range(2):
                            j = 2 * t + bj
                            uv = UV[:, h, j].rearrange("p g d -> p (g d)")
                            for k in range(NI):
                                q, bi = divmod(k, 2)
                                bank, at = divmod(k, PER)
                                o = po[:, h % 2, bank, at * 3 * W:(at + 1) * 3 * W]
                                nc.tensor.matmul(o[:, 0:2 * W], m1[:, u % NM, q, bi, bj], uv, start=j == 0 and at == 0,
                                                 stop=j == NT - 1, skip_group_check=True)
                                last = nc.tensor.matmul(o[:, 2 * W:3 * W], mb[:, t, q, bi, bj], uv[:, W:2 * W], start=False,
                                                        stop=j == NT - 1, skip_group_check=True)
                        last.then_inc(summed, 1)


def residual_norm(nc, tally, tag, x, OUT, elu, bias, gamma, beta, ident, Y, XT, XR):
    affine = gamma is not None
    norms = 2 if affine else 1
    xv = tokens(x)
    with ExitStack() as ctx:
        sb, ps, sem = spaces(nc, ctx, tag)
        EL = sb("EL", [P, NT, DM], F32) if elu else None
        BI, GA, BT = (sb(n, [P, DM], F32) for n in ("BI", "GA", "BT")) if affine else (None, None, None)
        EPT = sb("EPT", [P, 1], F32)
        XS = sb("XS", [P, 2, 2, DM], F32)
        TT = sb("TT", [P, 2, DM], F32)
        XN = sb("XN", [P, 2, 2, DM], F32)
        ST = sb("ST", [P, 2, 6], F32)
        MV = sb("MV", [P, 2, 2], F32)
        SD = sb("SDEV", [P, 2], F32)
        RS = sb("RS", [P, 2], F32)
        pt = ps("pt", [P, 2, 4, P], F32)
        n_const = 3 if affine else 0
        const_loaded, clipped, elu_done, added, stats, std, normed, turned, xt_ready, chain = (sem(n) for n in
            ("const_loaded", "clipped", "elu_done", "added", "stats", "std", "normed", "turned", "xt_ready", "chain"))
        kept = sem("kept")
        x_loaded = [sem(f"x_loaded{k}") for k in range(2)]
        block = ctx.enter_context(nc.Block())

        @block.sync
        def _(sp):
            if affine:
                for dst, src in ((BI, bias), (GA, gamma), (BT, beta)):
                    sp.dma_start(dst[:], src.rearrange("(a e) -> a e", a=1).broadcast_to([P, DM])).then_inc(const_loaded, 16)
            with sp.Fori(0, T // 2) as i:
                for k in range(2):
                    wait_apart(sp, tally, added, i * 2 + (k + 1))
                    sp.dma_start(XS[:, k], xv[:, bass.ds(i * 2 + k, 1)]).then_inc(x_loaded[k], 16)

        @block.scalar
        def _(act):
            act.sem_inc(xt_ready, 2)
            if elu:
                act.wait_ge(clipped, 1)
                nc.scalar.activation(EL[:], EL[:], ACT.Exp).then_inc(elu_done, 1)
            with act.Fori(0, T // 2) as i:
                for k in range(2):
                    for m in range(norms):
                        act.wait_ge(stats, i * (2 * norms) + (k * norms + m + 1))
                        nc.scalar.activation(SD[:], MV[:, :, 1], ACT.Sqrt, bias=EPT[:, 0:1]).then_inc(std, 1)
                    act.wait_ge(turned, i * 2 + (2 + k + 1))
                    nc.scalar.copy(XT[:, :, bass.ds(i * 4 + 2 * k, 2), :],
                                   pt[:, k].rearrange("p (c b) m -> p c b m", c=KC)).then_inc(xt_ready, 1)

        @block.gpsimd
        def _(pool):
            pool.sem_inc(kept, 2)
            with pool.Fori(0, T // 2) as i:
                for k in range(2):
                    pool.wait_ge(normed, i * 2 + (k + 1))
                    nc.gpsimd.tensor_copy(XR[:, bass.ds(i * 4 + 2 * k, 2), :], XN[:, k]).then_inc(kept, 1)

        @block.tensor
        def _(pe):
            pe.sem_inc(turned, 2)
            with pe.Fori(0, T // 2) as i:
                for k in range(2):
                    pe.wait_ge(normed, i * 2 + (k + 1))
                    pe.wait_ge(xt_ready, i * 2 + (k + 1))
                    for c in range(KC):
                        for b in range(2):
                            last = nc.tensor.transpose(pt[:, k, 2 * c + b, :], XN[:, k, b, c * P:(c + 1) * P], ident[:])
                    last.then_inc(turned, 1)

        @block.vector
        def _(dve):
            dve.sem_inc(added, 2)
            ch = Chain(dve, chain)
            ch.link(nc.vector.memset(EPT[:], EPS))
            if elu:
                nc.vector.tensor_scalar(EL[:], OUT[:], 0.0, None, ALU.min).then_inc(clipped, 1)
                dve.wait_ge(elu_done, 1)
            else:
                dve.wait_ge(const_loaded, 16 * n_const)
            base = ch.n
            links = 2 * (10 if affine else 4)
            with dve.Fori(0, T // 2) as i:
                ch = Chain(dve, chain, dve.snap(i * links + base))
                for k in range(2):
                    pair = bass.ds(i * 4 + 2 * k, 2)
                    dve.wait_ge(x_loaded[k], i * 16 + 16)
                    if elu:
                        ch.link(nc.vector.scalar_tensor_tensor(TT[:], EL[:, pair, :], -1.0, XS[:, k], ALU.add, ALU.add))
                        ch.link(nc.vector.scalar_tensor_tensor(Y[:, pair, :], OUT[:, pair, :], 0.0, TT[:], ALU.max, ALU.add))
                    else:
                        ch.link(nc.vector.tensor_tensor(TT[:], OUT[:, pair, :], BI[:].rearrange("p (a d) -> p a d", a=1).broadcast_to([P, 2, DM]), ALU.add))
                        ch.link(nc.vector.tensor_tensor(Y[:, pair, :], TT[:], XS[:, k], ALU.add))
                    dve.sem_inc(added, 1)
                    for m in range(norms):
                        last_norm = m == norms - 1
                        src = [Y[:, bass.ds(i * 4 + 2 * k + b, 1), :].rearrange("p a d -> p (a d)") if m == 0 else TT[:, b, :] for b in range(2)]
                        nc.vector.bn_stats(ST[:, 0, :], src[0])
                        ch.link(nc.vector.bn_stats(ST[:, 1, :], src[1]), tally=tally)
                        nc.vector.bn_aggr(MV[:, 0, :], ST[:, 0, :])
                        nc.vector.bn_aggr(MV[:, 1, :], ST[:, 1, :]).then_inc(stats, 1)
                        dve.wait_ge(std, i * (2 * norms) + (k * norms + m + 1))
                        ch.link(nc.vector.reciprocal(RS[:], SD[:]))
                        if last_norm:
                            dve.wait_ge(turned, i * 2 + (k + 1))
                            dve.wait_ge(kept, i * 2 + (k + 1))
                        for b in range(2):
                            dst = TT[:, b, :] if affine and not last_norm else XN[:, k, b, :]
                            ins = nc.vector.tensor_scalar(dst, src[b], MV[:, b, 0:1], RS[:, b:b + 1], ALU.subtract, ALU.mult)
                        if not last_norm or affine:
                            ch.link(ins)
                        else:
                            ins.then_inc(normed, 1)
                    if affine:
                        ga, bt = (v[:].rearrange("p (a d) -> p a d", a=1).broadcast_to([P, 2, DM]) for v in (GA, BT))
                        ch.link(nc.vector.tensor_tensor(TT[:], XN[:, k], ga, ALU.mult))
                        ch.link(nc.vector.tensor_tensor(XN[:, k], TT[:], bt, ALU.add))
                        dve.sem_inc(normed, 1)
                assert ch.n == links


def gate(nc, tally, tag, wg, bg, b2, ident, iota8, tri, ones, firsts, slots, Y, XT, XR, W12, SLOT, TEX, rows_in, y_rows):
    with ExitStack() as ctx:
        sb, ps, sem = spaces(nc, ctx, tag)
        WG = sb("WG", [P, KC, E], F32)
        BG = sb("BG", [P, E], F32)
        B2 = sb("B2", [E, DM], F32)
        LG = sb("LG", [P, NT, E], F32)
        MX = sb("MX", [P, NT, 8], F32)
        IX = sb("IX", [P, NT, 8], U32)
        IF = sb("IF", [P, NT, 2], F32)
        DF = sb("DF", [P, NT, 1], F32)
        EE = sb("EE", [P, NT, 1], F32)
        SM = sb("SM", [P, NT, 1], F32)
        CN = sb("CN", [P, NT, E], F32)
        TO = sb("TO", [P, NT, E], F32)
        PX = sb("PX", [P, 2, NT, E], F32)
        GE = sb("GE", [P, E, NT], F32)
        TL = sb("TL", [P, E], F32)
        EN = sb("EN", [P, 2, E], F32)
        BS = sb("BS", [P, E], F32)
        SF = sb("SF", [P, NT, 2], F32)
        O2 = sb("O2", [P, NT, 2, E], F32)
        TC = sb("TC", [1, TILES, E], F32)
        TF = sb("TF", [1, TILES], F32)
        OH = sb("OH", [P, NT, 2, E], F32)
        WB = sb("WB", [P, NT, E], F32)
        WT = sb("WT", [E, NT, P], F32)
        pl = ps("pl", [P, 512], F32)
        pw = ps("pw", [E, 2, 4, P], F32)
        pb = ps("pb", [P, 3, 2, DM], F32)
        pr = ps("pr", [P, 2, 512], F32)
        cleared, hot, ranked, slotted, scattered, stored, zero = (sem(n) for n in
            ("cleared", "hot", "ranked", "slotted", "scattered", "stored", "zero"))
        ZR = sb("ZR", [P, 8, DM], F32)
        const_loaded, logits, chain, diff, ex, weighed, wd_turned, wd_copied, summed, added = (sem(n) for n in
            ("const_loaded", "logits", "chain", "diff", "ex", "weighed", "wd_turned", "wd_copied", "summed", "added"))
        block = ctx.enter_context(nc.Block())

        @block.sync
        def _(sp):
            sp.dma_start(WG[:], wg.rearrange("(c p) e -> p c e", p=P)).then_inc(const_loaded, 16)
            sp.dma_start(BG[:], bg.rearrange("(a e) -> a e", a=1).broadcast_to([P, E])).then_inc(const_loaded, 16)
            sp.dma_start(B2[:], b2).then_inc(const_loaded, 16)
            sp.wait_ge(zero, 1)
            rz = rows_in.rearrange("(a b p) d -> a p b d", p=P, b=8)
            for a in range(TILES // 8):
                sp.dma_start(rz[a], ZR[:]).then_inc(cleared, 16)
            sp.wait_ge(added, T)
            sp.dma_start(y_rows, Y[:]).then_inc(stored, 16)
            sp.wait_ge(stored, 16)

        @block.gpsimd
        def _(pool):
            nc.gpsimd.memset(ZR[:], 0.0).then_inc(zero, 1)
            pool.wait_ge(slotted, 1)
            pool.wait_ge(cleared, 16 * (TILES // 8))
            for n in range(NT):
                for k in range(2):
                    nc.gpsimd.indirect_dma_start(rows_in, bass.IndirectOffsetOnAxis(SLOT[:, k, n:n + 1], 0),
                                                 XR[:, n, :], None).then_inc(scattered, 16)
            pool.wait_ge(scattered, 16 * 2 * NT)

        @block.tensor
        def _(pe):
            pe.wait_ge(const_loaded, 48)
            for n in range(NT):
                for c in range(KC):
                    last = nc.tensor.matmul(pl[:, n * E:(n + 1) * E], XT[:, c, n, :], WG[:, c, :], start=c == 0, stop=c == KC - 1)
            last.then_inc(logits, 1)
            pe.wait_ge(hot, 1)
            cn = CN[:].rearrange("p n e -> p (n e)")
            nc.tensor.matmul(pr[:, 0, 0:NT * E], tri[:], cn, start=True, stop=True)
            nc.tensor.matmul(pr[:, 1, 0:NT * E], ones[:], cn, start=True, stop=True).then_inc(ranked, 1)
            pe.wait_ge(weighed, 1)
            for q in range(4):
                if q:
                    pe.wait_ge(wd_copied, q)
                for n in range(8):
                    last = nc.tensor.transpose(pw[:, n // 4, n % 4, :], WB[:, 8 * q + n, :], ident[:])
                last.then_inc(wd_turned, 1)
            pe.wait_ge(wd_copied, 4)
            for t in range(T):
                if t >= 3:
                    pe.wait_ge(added, t - 2)
                for b in range(2):
                    last = nc.tensor.matmul(pb[:, t % 3, b, :], WT[:, 2 * t + b, :], B2[:], start=True, stop=True)
                last.then_inc(summed, 1)

        @block.scalar
        def _(act):
            act.wait_ge(diff, 1)
            nc.scalar.activation(EE[:], DF[:], ACT.Exp).then_inc(ex, 1)
            for q in range(4):
                act.wait_ge(wd_turned, q + 1)
                nc.scalar.copy(WT[:, 8 * q:8 * q + 8, :].rearrange("e (a n) m -> e a n m", a=2), pw[:]).then_inc(wd_copied, 1)

        @block.vector
        def _(dve):
            ch = Chain(dve, chain)
            dve.wait_ge(const_loaded, 48)
            dve.wait_ge(logits, 1)
            ch.link(nc.vector.tensor_tensor(LG[:], pl[:, 0:NT * E].rearrange("p (n e) -> p n e", e=E),
                                            BG[:].rearrange("p (a e) -> p a e", a=1).broadcast_to([P, NT, E]), ALU.add))
            for n in range(NT):
                ins = nc.vector.max(MX[:, n, :], LG[:, n, :])
            ch.link(ins)
            for n in range(NT):
                ins = nc.vector.max_index(IX[:, n, :], MX[:, n, :], LG[:, n, :])
            ch.link(ins)
            nc.vector.tensor_copy(IF[:], IX[:, :, 0:2])
            nc.vector.tensor_tensor(DF[:], MX[:, :, 1:2], MX[:, :, 0:1], ALU.subtract).then_inc(diff, 1)
            dve.wait_ge(ex, 1)
            ch.link(nc.vector.tensor_scalar(SM[:], EE[:], 1.0, None, ALU.add))
            ch.link(nc.vector.reciprocal(W12[:, :, 0:1], SM[:]))
            ch.link(nc.vector.tensor_tensor(W12[:, :, 1:2], EE[:], W12[:, :, 0:1], ALU.mult))
            iota_b = iota8[:].rearrange("p (a b e) -> p a b e", a=1, b=1).broadcast_to([P, NT, 2, E])
            ch.link(nc.vector.tensor_tensor(OH[:], iota_b, IF[:].rearrange("p n (k a) -> p n k a", a=1).broadcast_to([P, NT, 2, E]), ALU.is_equal))
            ch.link(nc.vector.tensor_tensor(CN[:], OH[:, :, 0, :], OH[:, :, 1, :], ALU.add))
            dve.sem_inc(hot, 1)
            ch.link(nc.vector.tensor_tensor(O2[:], OH[:], W12[:].rearrange("p n (k a) -> p n k a", a=1).broadcast_to([P, NT, 2, E]), ALU.mult))
            ch.link(nc.vector.tensor_tensor(WB[:], O2[:, :, 0, :], O2[:, :, 1, :], ALU.add))
            dve.sem_inc(weighed, 1)
            dve.wait_ge(ranked, 1)
            ch.link(nc.vector.tensor_copy(TO[:], pr[:, 1, 0:NT * E].rearrange("p (n e) -> p n e", e=E)))
            src = TO[:]
            for m, d in enumerate((1, 2, 4, 8, 16)):
                nc.vector.tensor_copy(PX[:, m % 2, 0:d, :], src[:, 0:d, :])
                ch.link(nc.vector.tensor_tensor(PX[:, m % 2, d:NT, :], src[:, d:NT, :], src[:, 0:NT - d, :], ALU.add))
                src = PX[:, m % 2]
            cnt = src[:, NT - 1, :].rearrange("p (e a) -> p e a", a=1).broadcast_to([P, E, NT])
            ch.link(nc.vector.tensor_tensor(GE[:], cnt, firsts[:].rearrange("p (a n) -> p a n", a=1).broadcast_to([P, E, NT]), ALU.is_gt))
            ch.link(nc.vector.tensor_reduce(TL[:], GE[:], X, ALU.add))
            es = TL[:]
            for m, d in enumerate((1, 2, 4)):
                nc.vector.tensor_copy(EN[:, m % 2, 0:d], es[:, 0:d])
                ch.link(nc.vector.tensor_tensor(EN[:, m % 2, d:E], es[:, d:E], es[:, 0:E - d], ALU.add))
                es = EN[:, m % 2]
            ch.link(nc.vector.tensor_tensor(BS[:], es, TL[:], ALU.subtract))
            ch.link(nc.vector.tensor_scalar(BS[:], BS[:], float(P), None, ALU.mult))
            ch.link(nc.vector.tensor_tensor(PX[:, 1], src, TO[:], ALU.subtract))
            ch.link(nc.vector.tensor_tensor(TO[:], PX[:, 1], pr[:, 0, 0:NT * E].rearrange("p (n e) -> p n e", e=E), ALU.add))
            ch.link(nc.vector.tensor_tensor(PX[:, 1], TO[:], BS[:].rearrange("p (a e) -> p a e", a=1).broadcast_to([P, NT, E]), ALU.add))
            for k in range(2):
                ch.link(nc.vector.tensor_tensor(O2[:, :, k, :], OH[:, :, k, :], PX[:, 1], ALU.mult))
            ch.link(nc.vector.tensor_reduce(SF[:], O2[:], X, ALU.add))
            ch.link(nc.vector.tensor_copy(SLOT[:].rearrange("p k n -> p n k"), SF[:]))
            dve.sem_inc(slotted, 1)
            ch.link(nc.vector.tensor_tensor(TC[:], slots[0:1].rearrange("p (t a) -> p t a", a=1).broadcast_to([1, TILES, E]),
                                            es[0:1].rearrange("p (a e) -> p a e", a=1).broadcast_to([1, TILES, E]), ALU.is_ge))
            ch.link(nc.vector.tensor_reduce(TF[:], TC[:], X, ALU.add))
            ch.link(nc.vector.tensor_scalar(TEX[:], TF[:], float(E - 1), None, ALU.min))
            for t in range(T):
                dve.wait_ge(summed, t + 1)
                nc.vector.tensor_tensor(Y[:, 2 * t:2 * t + 2, :], Y[:, 2 * t:2 * t + 2, :], pb[:, t % 3], ALU.add).then_inc(added, 1)


def experts(nc, tally, tag, HH, w1, b1, w2, ident, TEX, rows_in, rows_out):
    HT = HH // P
    HV = HT // 4
    with ExitStack() as ctx:
        sb, ps, sem = spaces(nc, ctx, tag)
        W1 = sb("W1", [P, E, KC, HH], F32)
        W2 = sb("W2", [P, E, HT, DM], F32)
        WS = sb("WS", [P, 2, KC, HH], F32)
        B1R = sb("B1R", [E * HT, P], F32)
        B1 = sb("B1", [P, E, HT, 1], F32)
        XS = sb("XS", [P, 2, DM], F32)
        XT = sb("XT", [P, 2, KC, P], F32)
        HB = sb("HB", [P, 2, 4, P], F32)
        GT = sb("GT", [P, 2, HT, P], F32)
        YS = sb("YS", [P, 2, DM], F32)
        px = ps("px", [P, 4, P], F32)
        p1 = ps("p1", [P, 2, 4, P], F32)
        py = ps("py", [P, 2, 512], F32)
        x_loaded = [sem(f"x_loaded{k}") for k in range(2)]
        y_stored = [sem(f"y_stored{k}") for k in range(2)]
        b1_loaded, b1_turned, b1_copied = sem("b1_loaded"), sem("b1_turned"), sem("b1_copied")
        placed = sem("placed")
        w_loaded, x_turned, x_copied, up, biased, gelued, down, copied = (sem(n) for n in
            ("w_loaded", "x_turned", "x_copied", "up", "biased", "gelued", "down", "copied"))
        block = ctx.enter_context(nc.Block())
        LOOP = TILES // 2
        C_XT, C_XC, C_UP, C_BI, C_GE, C_DN, C_CP, C_ST = 2, 1, 2 * HV, 2, 2, 2, 2, 16

        @block.gpsimd
        def _(pool):
            for e in range(E):
                pool.dma_start(W1[:, e], w1[e].rearrange("(c p) h -> p c h", p=P)).then_inc(w_loaded, 16)
                pool.dma_start(W2[:, e], w2[e].rearrange("(c p) d -> p c d", p=P)).then_inc(w_loaded, 16)
                pool.wait_ge(w_loaded, 32 * (e + 1))

        @block.sync
        def _(sp):
            sp.sem_inc(y_stored[0], C_ST)
            sp.sem_inc(y_stored[1], C_ST)
            sp.dma_start(B1R[:], b1.rearrange("e (h p) -> (e h) p", p=P)).then_inc(b1_loaded, 16)

            def load(s, k):
                wait_apart(sp, tally, x_turned, s + 1)
                sp.dma_start(XS[:, k], rows_in[bass.ds(s * P, P), :]).then_inc(x_loaded[k], 16)

            def store(s, k):
                wait_apart(sp, tally, copied, s + (C_CP + 1))
                sp.dma_start(rows_out[bass.ds(s * P, P), :], YS[:, k]).then_inc(y_stored[k], 16)

            for s in range(4):
                load(s, s % 2)
            store(0, 0)
            with sp.Fori(2, LOOP) as i:
                for k in range(2):
                    s = sp.snap(i * 2 + k)
                    load(s, k)
                    store(sp.snap(s - 3), 1 - k)
            store(TILES - 3, 1)
            store(TILES - 2, 0)
            store(TILES - 1, 1)
            for k in range(2):
                sp.wait_ge(y_stored[k], C_ST + 16 * LOOP)

        @block.tensor
        def _(pe):
            for sm, c in ((x_turned, C_XT), (up, C_UP), (down, C_DN)):
                pe.sem_inc(sm, c)
            pe.wait_ge(b1_loaded, 16)
            nc.tensor.transpose(py[:, 0, 0:E * HT], B1R[:], ident[0:E * HT, 0:E * HT]).then_inc(b1_turned, 1)

            def turn_part(s, k):
                pe.wait_ge(x_loaded[k], s * 8 + (16 - 8 * k))
                pe.wait_ge(x_copied, s + C_XC)
                for c in range(KC):
                    last = nc.tensor.transpose(px[:, c, :], XS[:, k, c * P:(c + 1) * P], ident[:])
                last.then_inc(x_turned, 1)

            def up_part(s, k):
                pe.wait_ge(placed, s + 1)
                pe.wait_ge(x_copied, s + (C_XC + 1))
                for v in range(HV):
                    pe.wait_ge(biased, s * HV + (v + 1))
                    for q in range(4):
                        for c in range(KC):
                            h = (4 * v + q) * P
                            last = nc.tensor.matmul(p1[:, v if HV == 2 else k, q, :], WS[:, k, c, h:h + P], XT[:, k, c, :], start=c == 0, stop=c == KC - 1)
                    last.then_inc(up, 1)

            def down_part(s, k):
                pe.wait_ge(gelued, s * HV + (C_GE + HV))
                pe.wait_ge(copied, s + 1)
                ex = pe.value_load(TEX[0:1, bass.ds(s, 1)], min_val=0, max_val=E - 1)
                for h in range(HT):
                    w = W2[:, bass.ds(ex, 1), h, :].rearrange("p a d -> p (a d)")
                    last = nc.tensor.matmul(py[:, k, 0:DM], GT[:, k, h, :], w, start=h == 0, stop=h == HT - 1)
                last.then_inc(down, 1)

            turn_part(0, 0)
            up_part(0, 0)
            turn_part(1, 1)
            pe.wait_ge(b1_copied, 1)
            with pe.Fori(0, LOOP - 1) as i:
                for k in (1, 0):
                    s = pe.snap(i * 2 + (2 - k))
                    up_part(s, k)
                    turn_part(pe.snap(s + 1), 1 - k)
                    down_part(pe.snap(s - 1), 1 - k)
            up_part(TILES - 1, 1)
            down_part(TILES - 2, 0)
            down_part(TILES - 1, 1)

        @block.scalar
        def _(act):
            act.sem_inc(x_copied, C_XC)
            act.sem_inc(gelued, C_GE)

            def x_part(s, k):
                act.wait_ge(x_turned, s + (C_XT + 1))
                act.wait_ge(up, s * HV + HV)
                nc.scalar.copy(XT[:, k], px[:, 0:KC, :]).then_inc(x_copied, 1)

            def gelu_part(s, k):
                act.wait_ge(down, s + 1)
                for v in range(HV):
                    act.wait_ge(biased, s * HV + (C_BI + v + 1))
                    nc.scalar.activation(GT[:, k, 4 * v:4 * v + 4, :], HB[:, v if HV == 2 else k], ACT.Gelu).then_inc(gelued, 1)

            x_part(0, 0)
            gelu_part(0, 0)
            x_part(1, 1)
            with act.Fori(0, LOOP - 1) as i:
                for k in (1, 0):
                    s = act.snap(i * 2 + (2 - k))
                    gelu_part(s, k)
                    x_part(act.snap(s + 1), 1 - k)
            gelu_part(TILES - 1, 1)

        @block.vector
        def _(dve):
            dve.sem_inc(biased, C_BI)
            dve.sem_inc(copied, C_CP)
            dve.wait_ge(b1_turned, 1)
            nc.vector.tensor_copy(B1[:].rearrange("p e h o -> p (e h o)"), py[:, 0, 0:E * HT]).then_inc(b1_copied, 1)
            dve.wait_ge(b1_copied, 1)

            def place_part(s, k):
                ex = dve.value_load(TEX[0:1, bass.ds(s, 1)], min_val=0, max_val=E - 1)
                dve.wait_ge(w_loaded, ex * 32 + 32)
                dve.wait_ge(up, s * HV + HV)
                nc.vector.tensor_copy(WS[:, k].rearrange("p c h -> p (c h)"),
                                      W1[:, bass.ds(ex, 1)].rearrange("p a c h -> p (a c h)")).then_inc(placed, 1)

            def bias_part(s, k):
                ex = dve.value_load(TEX[0:1, bass.ds(s, 1)], min_val=0, max_val=E - 1)
                for v in range(HV):
                    dve.wait_ge(gelued, s * HV + (v + 1))
                    dve.wait_ge(up, s * HV + (C_UP + v + 1))
                    b = v if HV == 2 else k
                    bias = B1[:, bass.ds(ex, 1), 4 * v:4 * v + 4, :].rearrange("p a h o -> p (a h) o").broadcast_to([P, 4, P])
                    nc.vector.tensor_tensor(HB[:, b], p1[:, b], bias, ALU.add).then_inc(biased, 1)

            def out_part(s, k):
                dve.wait_ge(y_stored[k], s * 8 + (C_ST - 8 * k))
                dve.wait_ge(down, s + (C_DN + 1))
                nc.vector.tensor_copy(YS[:, k], py[:, k, 0:DM]).then_inc(copied, 1)

            place_part(0, 0)
            bias_part(0, 0)
            place_part(1, 1)
            with dve.Fori(0, LOOP - 1) as i:
                for k in (1, 0):
                    s = dve.snap(i * 2 + (2 - k))
                    bias_part(s, k)
                    place_part(dve.snap(s + 1), 1 - k)
                    out_part(dve.snap(s - 1), 1 - k)
            bias_part(TILES - 1, 1)
            out_part(TILES - 2, 0)
            out_part(TILES - 1, 1)


def combine_experts(nc, tally, tag, y_rows, rows_out, SLOT, W12, dst):
    GR = 8
    TG = NT // GR
    with ExitStack() as ctx:
        sb, _, sem = spaces(nc, ctx, tag)
        Y = sb("Y", [P, NT, DM], F32)
        R = sb("R", [P, NT, 2, DM], F32)
        loaded = [sem(f"loaded{g}") for g in range(GR)]
        gathered = [sem(f"gathered{g}") for g in range(GR)]
        chain, stored = sem("chain"), sem("stored")
        block = ctx.enter_context(nc.Block())

        @block.gpsimd
        def _(pool):
            for n in range(NT):
                for k in range(2):
                    nc.gpsimd.indirect_dma_start(R[:, n, k, :], None, rows_out,
                                                 bass.IndirectOffsetOnAxis(SLOT[:, k, n:n + 1], 0)).then_inc(gathered[n // TG], 16)

        @block.sync
        def _(sp):
            for g in range(GR):
                sp.dma_start(Y[:, TG * g:TG * (g + 1)], y_rows[:, TG * g:TG * (g + 1)]).then_inc(loaded[g], 16)
            for g in range(GR):
                sp.wait_ge(chain, 2 * TG * (g + 1))
                sp.dma_start(tokens(dst)[:, 2 * g:2 * g + 2], Y[:, TG * g:TG * (g + 1), :].rearrange("p (t b) d -> p t b d", b=2)).then_inc(stored, 16)
            sp.wait_ge(stored, 16 * GR)

        @block.vector
        def _(dve):
            for g in range(GR):
                dve.wait_ge(loaded[g], 16)
                dve.wait_ge(gathered[g], 32 * TG)
                for k in range(2):
                    if k:
                        dve.wait_ge(chain, TG * (2 * g + 1))
                    for n in range(TG * g, TG * (g + 1)):
                        nc.vector.scalar_tensor_tensor(Y[:, n, :], R[:, n, k, :], W12[:, n, k:k + 1], Y[:, n, :],
                                                       ALU.mult, ALU.add).then_inc(chain, 1)


def program(nc, x, adj, L0_gnn_W, L0_gnn_a_src, L0_gnn_a_dst, L0_ffn_Wg, L0_ffn_bg, L0_ffn_W1, L0_ffn_b1, L0_ffn_W2, L0_ffn_b2,
            L1_gnn_W, L1_gnn_a_src, L1_gnn_a_dst, L1_gnn_bias, L1_ffn_gamma, L1_ffn_beta, L1_ffn_Wr, L1_ffn_br, L1_ffn_W1,
            L1_ffn_b1, L1_ffn_W2, L1_ffn_b2, out, stages=99):
    nc.disable_value_cache = True
    mask_t = nc.dram_tensor("mask_t", [P, T, 2 * N], U8).ap()
    x_mid = nc.dram_tensor("x_mid", [N, DM], F32).ap()
    layers = [
        dict(H=4, D=64, IB=512, x=x, dst=x_mid, w_rows=L0_gnn_W, w_cols=None, a=(L0_gnn_a_src, L0_gnn_a_dst), elu=True, bias=None,
             gamma=None, beta=None, wg=L0_ffn_Wg, bg=L0_ffn_bg, w1=L0_ffn_W1, b1=L0_ffn_b1, w2=L0_ffn_W2, b2=L0_ffn_b2, HH=1024),
        dict(H=8, D=32, IB=1024, x=x_mid, dst=out, w_rows=None, w_cols=L1_gnn_W, a=(L1_gnn_a_src, L1_gnn_a_dst), elu=False,
             bias=L1_gnn_bias, gamma=L1_ffn_gamma, beta=L1_ffn_beta, wg=L1_ffn_Wr, bg=L1_ffn_br, w1=L1_ffn_W1, b1=L1_ffn_b1,
             w2=L1_ffn_W2, b2=L1_ffn_b2, HH=512),
    ]
    with ExitStack() as top:
        sb0, _, sem0 = spaces(nc, top, "all")
        tally = sem0("tally")
        ident = sb0("ident", [P, P], F32)
        ident16 = sb0("ident16", [P, P], F16)
        eye = sb0("eye", [P, 4 * P], F8)
        iota8 = sb0("iota8", [P, E], F32)
        tri = sb0("tri", [P, P], F32)
        ones = sb0("ones", [P, P], F32)
        firsts = sb0("firsts", [P, NT], F32)
        slots = sb0("slots", [P, TILES], F32)
        W12 = sb0("W12", [P, NT, 2], F32)
        SLOT = sb0("SLOT", [P, 2, NT], U32)
        TEX = sb0("TEX", [1, TILES], mybir.dt.int32)
        y_rows = nc.dram_tensor("y_rows", [P, NT, DM], F32).ap()
        rows_in = nc.dram_tensor("rows_in", [TILES * P, DM], F32).ap()
        rows_out = nc.dram_tensor("rows_out", [TILES * P, DM], F32).ap()
        constants(nc, ident, ident16, eye, iota8, tri, ones, firsts, slots)
        transpose_mask(nc, tally, adj, mask_t, ident16)
        for n, L in enumerate(layers):
            tag, H, D = f"L{n}", L["H"], L["D"]
            if n >= stages:
                break
            with ExitStack() as layer:
                sbl, _, _ = spaces(nc, layer, tag)
                OUT = sbl("OUT", [P, NT, DM], F32)
                with ExitStack() as att:
                    sba, _, _ = spaces(nc, att, tag)
                    UV = sba("UV", [P, H, NT, 4, D + 1], F16)
                    NEGD, BIGD, AL, BE = (sba(v, [P, NT, H], F32) for v in ("NEGD", "BIGD", "AL", "BE"))
                    s_rows = nc.dram_tensor(f"{tag}_s_rows", [H, N], F32).ap()
                    project(nc, tally, tag + "p", H, D, L["x"], L["w_rows"], L["w_cols"], *L["a"], ident, s_rows, UV, NEGD, BIGD, AL, BE)
                    if n == 1:
                        add_diagonal(nc, tally, mask_t, eye)
                    attention(nc, tally, tag + "a", H, D, L["IB"], s_rows, mask_t, UV, NEGD, BIGD, AL, BE, OUT)
                Y = sbl("Y", [P, NT, DM], F32)
                XT = sbl("XT", [P, KC, NT, P], F32)
                XR = sbl("XR", [P, NT, DM], F32)
                residual_norm(nc, tally, tag + "r", L["x"], OUT, L["elu"], L["bias"], L["gamma"], L["beta"], ident, Y, XT, XR)
                gate(nc, tally, tag + "g", L["wg"], L["bg"], L["b2"], ident, iota8, tri, ones, firsts, slots, Y, XT, XR,
                     W12, SLOT, TEX, rows_in, y_rows)
            experts(nc, tally, tag + "e", L["HH"], L["w1"], L["b1"], L["w2"], ident, TEX, rows_in, rows_out)
            combine_experts(nc, tally, tag + "c", y_rows, rows_out, SLOT, W12, L["dst"] if stages > n + 1 else out)


_INS = ["x", "adj", "L0_gnn_W", "L0_gnn_a_src", "L0_gnn_a_dst", "L0_ffn_Wg", "L0_ffn_bg", "L0_ffn_W1", "L0_ffn_b1", "L0_ffn_W2",
        "L0_ffn_b2", "L1_gnn_W", "L1_gnn_a_src", "L1_gnn_a_dst", "L1_gnn_bias", "L1_ffn_gamma", "L1_ffn_beta", "L1_ffn_Wr",
        "L1_ffn_br", "L1_ffn_W1", "L1_ffn_b1", "L1_ffn_W2", "L1_ffn_b2"]


def kernel(**inputs):
    from concourse import bacc
    from concourse.bass_utils import run_bass_kernel_spmd

    nc = bacc.Bacc("TRN2", target_bir_lowering=False, num_devices=1)
    arrays, args = {}, {}
    for name in _INS:
        a = np.ascontiguousarray(inputs[name])
        arrays[f"in_{name}"] = a
        args[name] = nc.dram_tensor(f"in_{name}", a.shape, mybir.dt.from_np(a.dtype), kind="ExternalInput").ap()
    out = nc.dram_tensor("out", [N, DM], F32, kind="ExternalOutput").ap()
    program(nc, out=out, **args)
    r = run_bass_kernel_spmd(nc, [arrays], core_ids=[0])
    return r.results[0]["out"]
```
